# Optimizing a Trainium2 kernel written in Bass

```python
import numpy as np
import jax
import jax.numpy as jnp

def _softmax(x, axis=-1):
    return jax.nn.softmax(x, axis=axis)

def _gelu(x):
    return jax.nn.gelu(x, approximate=True)

def _silu(x):
    return jax.nn.silu(x)

def _sigmoid(x):
    return jax.nn.sigmoid(x)

def _layernorm(x, axis=-1, eps=1e-05):
    m = jnp.mean(x, axis=axis, keepdims=True)
    v = jnp.var(x, axis=axis, keepdims=True)
    return (x - m) / jnp.sqrt(v + eps)

def _scatter_add(tgt, idx, src, axis=0):
    return tgt.at[idx].add(src)

def _segment_sum(src, seg, n):
    return jax.ops.segment_sum(src, seg, n)
kernel_name = 'mk_gnn_resnorm_d1_gnn_r32_f2cac2'

def setup_inputs(seed: int=0):
    np.random.seed(seed)
    _w = jnp.asarray

    def _rec_inputs():
        import jax
        import jax.numpy as jnp
        _gk = jax.random.key(seed)
        x = -0.000202 + 1 * jax.random.normal(jax.random.fold_in(_gk, 1), (50000, 256), jnp.float32)
        src = jax.random.randint(jax.random.fold_in(_gk, 2), (50000,), 0, 50000, jnp.int32)
        dst = jnp.minimum((50000 * jax.random.uniform(jax.random.fold_in(_gk, 3), (50000,)) ** 2.0).astype(jnp.int32), 49999)
        _o = jnp.argsort(dst, stable=True)
        src = src[_o]
        dst = dst[_o]
        edge_attr_64 = -5.3897e-05 + 0.999841 * jax.random.normal(jax.random.fold_in(_gk, 12), (50000, 64), jnp.float32)
        edge_weight1 = jax.random.uniform(jax.random.fold_in(_gk, 13), (50000, 1), jnp.float32, 0.0, 0.999998)
        return (x, src, dst, edge_attr_64, edge_weight1)
    x, src, dst, edge_attr_64, edge_weight1 = _rec_inputs()

    def _L0_gnn_setup():
        import jax, jax.numpy as jnp
        import numpy as np
        LOG2 = float(np.log(2.0))

        def ssp(x):
            return jax.nn.softplus(x) - LOG2
        N_ATOMS, N_EDGES, N_HF, N_RBF = (25000, 12500, 256, 64)
        key = jax.random.key(seed)
        ks = jax.random.split(key, 16)
        s = 1.0 / np.sqrt(N_HF)
        sr = 1.0 / np.sqrt(N_RBF)
        return {'x': jax.random.normal(ks[0], (N_ATOMS, N_HF), jnp.float32), 'rbf': jax.random.normal(ks[1], (N_EDGES, N_RBF), jnp.float32), 'dist_cut': jax.random.uniform(ks[2], (N_EDGES, 1), jnp.float32), 'idx_i': jax.random.randint(ks[3], (N_EDGES,), 0, N_ATOMS), 'idx_j': jax.random.randint(ks[4], (N_EDGES,), 0, N_ATOMS), 'W_in2f': jax.random.normal(ks[5], (N_HF, N_HF), jnp.float32) * s, 'Wf1': jax.random.normal(ks[6], (N_RBF, N_HF), jnp.float32) * sr, 'bf1': jnp.zeros((N_HF,), jnp.float32), 'Wf2': jax.random.normal(ks[7], (N_HF, N_HF), jnp.float32) * s, 'bf2': jnp.zeros((N_HF,), jnp.float32), 'Wo1': jax.random.normal(ks[8], (N_HF, N_HF), jnp.float32) * s, 'bo1': jnp.zeros((N_HF,), jnp.float32), 'Wo2': jax.random.normal(ks[9], (N_HF, N_HF), jnp.float32) * s, 'bo2': jnp.zeros((N_HF,), jnp.float32)}
    _L0_gnn_all = _L0_gnn_setup()
    _L0_gnn_in = {k: v for k, v in _L0_gnn_all.items() if k in ('W_in2f', 'Wf1', 'bf1', 'Wf2', 'bf2', 'Wo1', 'bo1', 'Wo2', 'bo2')}
    del _L0_gnn_all
    return {'x': x, 'src': src, 'dst': dst, 'edge_attr_64': edge_attr_64, 'edge_weight1': edge_weight1, 'L0_gnn_W_in2f': _L0_gnn_in['W_in2f'], 'L0_gnn_Wf1': _L0_gnn_in['Wf1'], 'L0_gnn_bf1': _L0_gnn_in['bf1'], 'L0_gnn_Wf2': _L0_gnn_in['Wf2'], 'L0_gnn_bf2': _L0_gnn_in['bf2'], 'L0_gnn_Wo1': _L0_gnn_in['Wo1'], 'L0_gnn_bo1': _L0_gnn_in['bo1'], 'L0_gnn_Wo2': _L0_gnn_in['Wo2'], 'L0_gnn_bo2': _L0_gnn_in['bo2']}

def reference(x, src, dst, edge_attr_64, edge_weight1, L0_gnn_W_in2f, L0_gnn_Wf1, L0_gnn_bf1, L0_gnn_Wf2, L0_gnn_bf2, L0_gnn_Wo1, L0_gnn_bo1, L0_gnn_Wo2, L0_gnn_bo2):
    import jax
    import jax.numpy as jnp

    def _L0_gnn_ref(x, rbf, dist_cut, idx_i, idx_j, W_in2f, Wf1, bf1, Wf2, bf2, Wo1, bo1, Wo2, bo2):
        import jax, jax.numpy as jnp
        import numpy as np
        LOG2 = float(np.log(2.0))

        def ssp(x):
            return jax.nn.softplus(x) - LOG2
        N_ATOMS, N_EDGES, N_HF, N_RBF = (25000, 12500, 256, 64)
        n_atoms = x.shape[0]
        h = x @ W_in2f
        Wij = ssp(rbf @ Wf1 + bf1) @ Wf2 + bf2
        Wij = Wij * dist_cut
        x_ij = h[idx_j] * Wij
        m = jax.ops.segment_sum(x_ij, idx_i, num_segments=n_atoms)
        m = ssp(m @ Wo1 + bo1) @ Wo2 + bo2
        return x + m
    x = _layernorm(x + _L0_gnn_ref(x, edge_attr_64, edge_weight1, src, dst, L0_gnn_W_in2f, L0_gnn_Wf1, L0_gnn_bf1, L0_gnn_Wf2, L0_gnn_bf2, L0_gnn_Wo1, L0_gnn_bo1, L0_gnn_Wo2, L0_gnn_bo2), axis=-1)
    return x

_drawn_inputs = setup_inputs


def setup_inputs(seed=0):
    import zlib

    import numpy as np

    out = dict(_drawn_inputs(seed))
    spreads = {'L0_gnn_bf1': (0.0, 0.8),
     'L0_gnn_bf2': (0.0, 0.509),
     'L0_gnn_bo1': (0.0, 0.336),
     'L0_gnn_bo2': (0.0, 0.1)}
    factors = {}
    for name, (base, spread) in spreads.items():
        noise = np.random.default_rng([zlib.crc32(name.encode()), seed]).standard_normal(out[name].shape)
        drawn = base * np.exp(spread * noise) if base else spread * noise
        out[name] = jnp.asarray(drawn.astype(out[name].dtype))
    for name, factor in factors.items():
        out[name] = (out[name] * factor).astype(out[name].dtype)
    return out
```

```python
from contextlib import ExitStack

import concourse.bass as bass
from concourse import mybir

ALU = mybir.AluOpType
ACT = mybir.ActivationFunctionType
F32 = mybir.dt.float32
I32 = mybir.dt.int32

P = 128
R = 4
LOG2 = 0.6931471805599453
EXP_CAP = 40.0
EPS = 1e-5


class Group:

    def __init__(self, number, parity, nth, rows):
        self.n, self.par, self.nth, self.rows = number, parity, nth, rows
        self.p = rows // R


def wait(eng, sem, value):
    if isinstance(value, int) and value <= 0:
        return
    eng.wait_ge(sem, value)


def build(nc, t, out):
    N, D = t["x"].shape
    E = t["src"].shape[0]
    A = t["edge_attr_64"].shape[1]
    H = D // P
    ROWS = R * P
    assert D == 2 * P and 2 * A == P and E == N and E % R == 0
    G = -(-E // ROWS)
    TAIL = E - (G - 1) * ROWS
    PEEL = 3 if G % 2 == 0 else 2
    ROUNDS = (G - 1 - PEEL) // 2

    def group(n):
        return Group(n, n % 2, n // 2 + 1, ROWS if n < G - 1 else TAIL)

    def looped(i, u, back=0):
        k = PEEL + u - back
        return Group(i * 2 + k, k % 2, i + (k // 2 + 1), ROWS)

    acc = nc.dram_tensor("acc", [N + P, D], F32, kind="Internal").ap()

    with ExitStack() as ctx:
        def sb(name, shape, dt=F32):
            return ctx.enter_context(nc.sbuf_tensor(name, shape, dt))

        def sem(name):
            return ctx.enter_context(nc.semaphore(name))

        bank = [ctx.enter_context(nc.psum_tensor(f"bank{i}", [P, 512], F32)) for i in range(8)]

        ident = sb("ident", [P, P])
        below = sb("below", [P, P])
        w_in, wf2, wo1, wo2 = (sb(n, [P, H, D]) for n in ("w_in", "wf2", "wo1", "wo2"))
        wf1 = sb("wf1", [P, D])
        bf1, bo1 = sb("bf1", [P, H]), sb("bo1", [P, H])
        bf1s, bo1s = sb("bf1s", [P, H]), sb("bo1s", [P, H])
        bf2b, bo2h = sb("bf2b", [P, D]), sb("bo2h", [P, D])
        rows_i = sb("rows_i", [P, 2, ROWS], I32)
        rows_f = sb("rows_f", [P, 3, ROWS])
        src_t, dst_t, wgt_t = (sb(n, [P, R, G]) for n in ("src_t", "dst_t", "wgt_t"))
        spare_i = sb("spare_i", [P, 1], I32)
        spare_f = sb("spare_f", [P, 1])
        to_spare = sb("to_spare", [P, R, G])
        zeros = sb("zeros", [P, 30 * D])
        half = sb("half", [P, 1])

        attr = sb("attr", [P, 2, R * A])
        srcb = sb("srcb", [P, 2, ROWS], I32)
        xg = [[sb(f"xg{u}{r}", [P, D]) for r in range(R)] for u in range(2)]
        dst_ix = [[sb(f"dst_ix{u}{r}", [P, 1], I32) for r in range(R)] for u in range(2)]
        src_ix = [[sb(f"src_ix{u}{r}", [P, 1], I32) for r in range(R)] for u in range(2)]
        x_t = sb("x_t", [P, 2, 2, H, 2, P])
        a_t = sb("a_t", [P, 2, P])
        capped = sb("capped", [P, 2, 512])
        expz = sb("expz", [P, 2, 512])
        lnz = sb("lnz", [P, 2, 512])
        ssp = sb("ssp", [P, 2, 2, H, 2, P])
        same = sb("same", [P, 2, R, P])
        junk = sb("junk", [P, R, P])
        earlier = sb("earlier", [P, 2, R])
        move = sb("move", [P, R])
        filt = sb("filt", [P, 2, D])
        msg = sb("msg", [P, R, D])
        sum_t = sb("sum_t", [P, 2, 2, H, P])
        y = [sb(f"y{q}", [P, 2 * D]) for q in range(2)]

        m_in = sb("m_in", [P, 2, R, D])
        x_in = sb("x_in", [P, 2, R, D])
        xb = sb("xb", [P, 2, R, D])
        ssp2 = sb("ssp2", [P, 2, H, R, P])
        res = sb("res", [P, 2, R, D])
        stats = sb("stats", [P, 2, R, 6])
        mv = sb("mv", [P, 2, R, 2])
        veps = sb("veps", [P, 2, R])
        rstd = sb("rstd", [P, 2, R])
        neg_half = sb("neg_half", [P, R])
        nmr = sb("nmr", [P, 2, R])
        normed = sb("normed", [P, 2, R, D])

        dve_own = sem("dve_own")
        const_in = sem("const_in")
        rows_in = sem("rows_in")
        rows_zero = sem("rows_zero")
        rows_cast = sem("rows_cast")
        made = sem("made")
        cleared = sem("cleared")
        tab_ps = sem("tab_ps")
        tab_sb = sem("tab_sb")
        attr_in = [sem(f"attr_in{u}") for u in range(2)]
        srcb_in = [sem(f"srcb_in{u}") for u in range(2)]
        xg_in = [[sem(f"xg_in{u}{r}") for r in range(R)] for u in range(2)]
        added = sem("added")
        dst_ready = sem("dst_ready")
        src_ready = sem("src_ready")
        same_ready = sem("same_ready")
        earlier_ready = sem("earlier_ready")
        move_ready = sem("move_ready")
        xt_ps, xt_sb = sem("xt_ps"), sem("xt_sb")
        at_ps, at_sb = sem("at_ps"), sem("at_sb")
        z_ps = sem("z_ps")
        cap_ready, exp_ready, ln_ready, ssp_ready = (sem(n) for n in ("cap_ready", "exp_ready", "ln_ready", "ssp_ready"))
        hw_ps = sem("hw_ps")
        filt_ready, msg_ready = sem("filt_ready"), sem("msg_ready")
        sum_ps, sum_sb = sem("sum_ps"), sem("sum_sb")
        y_ps, y_sb = sem("y_ps"), sem("y_sb")
        pool_step, sp_step, dve_step = sem("pool_step"), sem("sp_step"), sem("dve_step")
        m_got = [sem(f"m_got{u}") for u in range(2)]
        x_got = [sem(f"x_got{u}") for u in range(2)]
        mt_ps = sem("mt_ps")
        cap2, exp2, ln2, ssp2_ready = (sem(n) for n in ("cap2", "exp2", "ln2", "ssp2_ready"))
        xb_ready = sem("xb_ready")
        o_ps = sem("o_ps")
        res_ready, stat_ready, mv_ready, veps_ready, rstd_ready, nmr_ready = (
            sem(n) for n in ("res_ready", "stat_ready", "mv_ready", "veps_ready", "rstd_ready", "nmr_ready"))
        norm_ready = sem("norm_ready")
        stored = [sem(f"stored{u}") for u in range(2)]

        block = ctx.enter_context(nc.Block())

        CONSTS = 12
        CLEARS = N // P // 30
        assert N // P % 30 == 0

        def rows_of(ap, g):
            return ap[bass.ds(g.n * ROWS, g.rows)]

        def col(table, r, g, p=P):
            return table[0:p, r, bass.ds(g.n, 1)]

        @block.sync
        def _(sp):
            for w, name in ((w_in, "L0_gnn_W_in2f"), (wf2, "L0_gnn_Wf2"), (wo1, "L0_gnn_Wo1"), (wo2, "L0_gnn_Wo2")):
                sp.dma_start(w[:], t[name].rearrange("(h p) n -> p h n", p=P)).then_inc(const_in, 16)
            for k in range(2):
                sp.dma_start(wf1[k * A:(k + 1) * A, :], t["L0_gnn_Wf1"]).then_inc(const_in, 16)
            for b, name in ((bf1, "L0_gnn_bf1"), (bo1, "L0_gnn_bo1")):
                for h in range(H):
                    sp.dma_start(b[:, h:h + 1], t[name][h * P:(h + 1) * P].rearrange("(p a) -> p a", a=1)).then_inc(const_in, 16)
            for b, name in ((bf2b, "L0_gnn_bf2"), (bo2h, "L0_gnn_bo2")):
                sp.dma_start(b[:], t[name].partition_broadcast(P)).then_inc(const_in, 16)
            sp.wait_ge(rows_zero, 1)
            for k, name in enumerate(("src", "dst")):
                sp.dma_start(rows_i[0:G - 1, k, :], t[name][0:(G - 1) * ROWS].rearrange("(g e) -> g e", e=ROWS)).then_inc(rows_in, 16)
                sp.dma_start(rows_i[G - 1:G, k, 0:TAIL], t[name][(G - 1) * ROWS:E].rearrange("(g e) -> g e", e=TAIL)).then_inc(rows_in, 16)
            flat = t["edge_weight1"].rearrange("e a -> (e a)")
            sp.dma_start(rows_f[0:G - 1, 2, :], flat[0:(G - 1) * ROWS].rearrange("(g e) -> g e", e=ROWS)).then_inc(rows_in, 16)
            sp.dma_start(rows_f[G - 1:G, 2, 0:TAIL], flat[(G - 1) * ROWS:E].rearrange("(g e) -> g e", e=TAIL)).then_inc(rows_in, 16)

            def load(g):
                wait(sp, at_ps, g.n - 1)
                sp.sem_inc(sp_step, 1)
                sp.dma_start(attr[0:g.p, g.par, :], rows_of(t["edge_attr_64"], g).rearrange("(p r) a -> p (r a)", r=R)).then_inc(attr_in[g.par], 16)
                wait(sp, same_ready, (g.n - 1) * R)
                sp.sem_inc(sp_step, 1)
                sp.dma_start(srcb[:, g.par, 0:g.rows], rows_of(t["src"], g).partition_broadcast(P)).then_inc(srcb_in[g.par], 16)

            for n in range(PEEL):
                load(group(n))
            with sp.Fori(0, ROUNDS) as i:
                for u in range(2):
                    load(looped(i, u))
            load(group(G - 1))

            sp.wait_ge(added, 16 * R * G)

            def fetch(g):
                wait(sp, mt_ps, (g.n - 1) * H)
                sp.sem_inc(sp_step, 1)
                sp.dma_start(m_in[0:g.p, g.par].rearrange("p r d -> p (r d)"), rows_of(acc, g).rearrange("(p r) d -> p (r d)", r=R)).then_inc(m_got[g.par], 16)
                wait(sp, xb_ready, g.n - 1)
                sp.sem_inc(sp_step, 1)
                sp.dma_start(x_in[0:g.p, g.par].rearrange("p r d -> p (r d)"), rows_of(t["x"], g).rearrange("(p r) d -> p (r d)", r=R)).then_inc(x_got[g.par], 16)

            def store(g):
                wait(sp, norm_ready, g.n + 1)
                sp.sem_inc(sp_step, 1)
                sp.dma_start(rows_of(out, g).rearrange("(p r) d -> p (r d)", r=R), normed[0:g.p, g.par].rearrange("p r d -> p (r d)")).then_inc(stored[g.par], 16)

            fetch(group(0))
            fetch(group(1))
            for n in range(2, PEEL):
                fetch(group(n))
                store(group(n - 2))
            with sp.Fori(0, ROUNDS) as i:
                for u in range(2):
                    fetch(looped(i, u))
                    store(looped(i, u, 2))
            fetch(group(G - 1))
            for n in range(G - 3, G):
                store(group(n))
            for u in range(2):
                sp.wait_ge(stored[u], 16 * len(range(u, G, 2)))

        @block.gpsimd
        def _(pool):
            pool.memset(ident[:], 0.0).then_inc(pool_step, 1)
            pool.memset(below[:], 1.0).then_inc(pool_step, 1)
            pool.memset(neg_half[:], -0.5).then_inc(made, 1)
            pool.iota(spare_i[:], [[0, 1]], base=N, channel_multiplier=1).then_inc(made, 1)
            pool.wait_ge(pool_step, 2)
            pool.affine_select(out=ident[:], in_=ident[:], compare_op=ALU.not_equal, fill=1.0, base=0,
                               pattern=[[-1, P]], channel_multiplier=1).then_inc(made, 1)
            pool.affine_select(out=below[:], in_=below[:], compare_op=ALU.is_gt, fill=0.0, base=0,
                               pattern=[[-1, P]], channel_multiplier=1).then_inc(made, 1)

            def gather(g, r):
                wait(pool, dst_ready, g.n + 1)
                wait(pool, xt_ps, (g.n - 1) * 2)
                pool.sem_inc(pool_step, 1)
                pool.indirect_dma_start(xg[g.par][r][0:g.p, :], None, t["x"],
                                        bass.IndirectOffsetOnAxis(ap=dst_ix[g.par][r][0:g.p, :], axis=0)).then_inc(xg_in[g.par][r], 16)

            def scatter(g, r):
                wait(pool, src_ready, g.n + 1)
                wait(pool, y_sb, g.n * 2 + r // 2 + 1)
                wait(pool, added, (g.n * R + r) * 16)
                pool.sem_inc(pool_step, 1)
                pool.indirect_dma_start(acc, bass.IndirectOffsetOnAxis(ap=src_ix[g.par][r][0:g.p, :], axis=0),
                                        y[r // 2][0:g.p, (r % 2) * D:(r % 2 + 1) * D], None, compute_op=ALU.add).then_inc(added, 16)

            def step(ahead, behind, last):
                if ahead is not None:
                    gather(ahead, 0)
                if last is not None:
                    scatter(last, 2)
                if ahead is not None:
                    gather(ahead, 1)
                if last is not None:
                    scatter(last, 3)
                if ahead is not None:
                    gather(ahead, 2)
                    gather(ahead, 3)
                if behind is not None:
                    scatter(behind, 0)
                    scatter(behind, 1)

            step(group(0), None, None)
            step(group(1), None, None)
            pool.wait_ge(cleared, 16 * (CLEARS + 1))
            for n in range(2, PEEL):
                step(group(n), group(n - 2), group(n - 3) if n > 2 else None)
            with pool.Fori(0, ROUNDS) as i:
                for u in range(2):
                    step(looped(i, u), looped(i, u, 2), looped(i, u, 3))
            step(group(G - 1), group(G - 3), group(G - 4))
            step(None, group(G - 2), group(G - 3))
            step(None, group(G - 1), group(G - 2))
            step(None, None, group(G - 1))

            def lift(g):
                pool.wait_ge(x_got[g.par], g.nth * 16)
                wait(pool, res_ready, (g.n - 1) * 2)
                pool.tensor_tensor(xb[0:g.p, g.par], x_in[0:g.p, g.par],
                                   bo2h[0:g.p, :].unsqueeze(1).broadcast_to([g.p, R, D]), ALU.add).then_inc(xb_ready, 1)

            def root(g):
                pool.wait_ge(veps_ready, g.n + 1)
                wait(pool, norm_ready, g.n - 1)
                pool.tensor_tensor(rstd[0:g.p, g.par], veps[0:g.p, g.par], neg_half[0:g.p], ALU.pow).then_inc(rstd_ready, 1)

            lift(group(0))
            for n in range(1, PEEL):
                lift(group(n))
                root(group(n - 1))
            with pool.Fori(0, ROUNDS) as i:
                for u in range(2):
                    lift(looped(i, u))
                    root(looped(i, u, 1))
            lift(group(G - 1))
            root(group(G - 2))
            root(group(G - 1))

        @block.tensor
        def _(pe):
            pe.wait_ge(made, 4)
            pe.wait_ge(rows_cast, 1)
            for k in range(3):
                if k == 2:
                    pe.wait_ge(rows_in, 16 * 6)
                for r in range(R):
                    last = pe.transpose(bank[k][:, r * G:(r + 1) * G], rows_f[0:G, k, r::R], ident[0:G, 0:G])
                last.then_inc(tab_ps, 1)
            pe.wait_ge(const_in, 16 * CONSTS)
            pe.wait_ge(tab_sb, 1)

            def turn(g):
                for q in range(2):
                    for k in range(2):
                        pe.wait_ge(xg_in[g.par][2 * q + k], g.nth * 16)
                    wait(pe, xt_sb, (g.n - 1) * 2 + q + 1)
                    for h in range(H):
                        for k in range(2):
                            last = pe.transpose(bank[q][:, (h * 2 + k) * P:(h * 2 + k) * P + g.p],
                                                xg[g.par][2 * q + k][0:g.p, h * P:(h + 1) * P], ident[0:g.p, 0:g.p])
                    last.then_inc(xt_ps, 1)
                pe.wait_ge(attr_in[g.par], g.nth * 16)
                wait(pe, ssp_ready, g.n * 2)
                for q in range(2):
                    last = pe.transpose(bank[2][:, q * P:q * P + g.p], attr[0:g.p, g.par, q * P:(q + 1) * P], ident[0:g.p, 0:g.p])
                last.then_inc(at_ps, 1)

            def filter1(g):
                pe.wait_ge(at_sb, g.n + 1)
                for h in range(H):
                    for k in range(2):
                        o = bank[2 + k][:, h * 2 * P:(h + 1) * 2 * P].rearrange("m (q e) -> m q e", q=2)
                        last = pe.matmul(o[:, :, 0:g.p], wf1[k * A:(k + 1) * A, h * P:(h + 1) * P],
                                         a_t[k * A:(k + 1) * A, :, 0:g.p], start=True, stop=True)
                last.then_inc(z_ps, 1)

            def h_and_w(g, r):
                q, k = r // 2, r % 2
                pe.wait_ge(xt_sb, g.n * 2 + q + 1)
                pe.wait_ge(ssp_ready, g.n * 2 + 2)
                wait(pe, msg_ready, g.n * R + r - 1)
                o = bank[4 + k]
                for h in range(H):
                    pe.matmul(o[0:g.p, 0:D], x_t[:, g.par, q, h, k, 0:g.p], w_in[:, h, :], start=h == 0, stop=h == H - 1)
                for h in range(H):
                    last = pe.matmul(o[0:g.p, D:2 * D], ssp[:, g.par, k, h, q, 0:g.p], wf2[:, h, :], start=h == 0, stop=h == H - 1)
                last.then_inc(hw_ps, 1)

            def summed(g, q):
                pe.wait_ge(msg_ready, g.n * R + 2 * q + 2)
                pe.wait_ge(same_ready, g.n * R + R)
                wait(pe, sum_sb, g.n * 2 + q)
                for k in range(2):
                    for h in range(H):
                        c = (k * H + h) * P
                        last = pe.matmul(bank[6][:, c:c + g.p], msg[0:g.p, 2 * q + k, h * P:(h + 1) * P],
                                         same[0:g.p, g.par, 2 * q + k, 0:g.p], start=True, stop=True)
                last.then_inc(sum_ps, 1)

            def out1(g, q):
                pe.wait_ge(sum_sb, g.n * 2 + q + 1)
                wait(pe, y_sb, g.n * 2 + q)
                for k in range(2):
                    for h in range(H):
                        last = pe.matmul(bank[7][0:g.p, k * D:(k + 1) * D], sum_t[:, q, k, h, 0:g.p],
                                         wo1[:, h, :], start=h == 0, stop=h == H - 1)
                last.then_inc(y_ps, 1)

            def step(ahead, behind, last):
                if ahead is not None:
                    turn(ahead)
                if last is not None:
                    out1(last, 1)
                if behind is not None:
                    h_and_w(behind, 0)
                    h_and_w(behind, 1)
                if ahead is not None:
                    filter1(ahead)
                if behind is not None:
                    h_and_w(behind, 2)
                    summed(behind, 0)
                    h_and_w(behind, 3)
                    out1(behind, 0)
                    summed(behind, 1)

            step(group(0), None, None)
            step(group(1), group(0), None)
            for n in range(2, PEEL):
                step(group(n), group(n - 1), group(n - 2))
            with pe.Fori(0, ROUNDS) as i:
                for u in range(2):
                    step(looped(i, u), looped(i, u, 1), looped(i, u, 2))
            step(group(G - 1), group(G - 2), group(G - 3))
            step(None, group(G - 1), group(G - 2))
            out1(group(G - 1), 1)

            def turn2(g):
                pe.wait_ge(m_got[g.par], g.nth * 16)
                for h in range(H):
                    wait(pe, ssp2_ready, (g.n - 1) * H + h - H + 1)
                    b = bank[2 * g.par + h]
                    for r in range(R):
                        last = pe.transpose(b[:, r * P:r * P + g.p], m_in[0:g.p, g.par, r, h * P:(h + 1) * P], ident[0:g.p, 0:g.p])
                    last.then_inc(mt_ps, 1)

            def out2(g):
                pe.wait_ge(ssp2_ready, g.n * H + H)
                for q in range(2):
                    wait(pe, res_ready, (g.n - 1) * 2 - 1 + q)
                    b = bank[4 + 2 * g.par + q]
                    for k in range(2):
                        for h in range(H):
                            last = pe.matmul(b[0:g.p, k * D:(k + 1) * D], ssp2[:, g.par, h, 2 * q + k, 0:g.p], wo2[:, h, :],
                                             start=h == 0, stop=h == H - 1)
                    last.then_inc(o_ps, 1)

            turn2(group(0))
            for n in range(1, PEEL):
                turn2(group(n))
                out2(group(n - 1))
            with pe.Fori(0, ROUNDS) as i:
                for u in range(2):
                    turn2(looped(i, u))
                    out2(looped(i, u, 1))
            turn2(group(G - 1))
            out2(group(G - 2))
            out2(group(G - 1))

        @block.scalar
        def _(act):
            act.preload_act_table_set("natural_log_exp_and_others")
            act.wait_ge(rows_zero, 1)
            for c in range(CLEARS):
                act.dma_start(acc[c * 30 * P:(c + 1) * 30 * P, :].rearrange("(p k) d -> p (k d)", k=30), zeros[:]).then_inc(cleared, 16)
            rest = N + P - CLEARS * 30 * P
            act.dma_start(acc[CLEARS * 30 * P:N + P, :].rearrange("(p k) d -> p (k d)", k=2), zeros[0:rest // 2, 0:2 * D]).then_inc(cleared, 16)

            def keep(g):
                for q in range(2):
                    act.wait_ge(xt_ps, g.n * 2 + q + 1)
                    wait(act, hw_ps, (g.n - 1) * R)
                    act.activation(x_t[:, g.par, q].rearrange("f h k e -> f (h k) e")[:, :, 0:g.p],
                                   bank[q][:].rearrange("f (b e) -> f b e", b=4)[:, :, 0:g.p], ACT.Copy).then_inc(xt_sb, 1)
                act.wait_ge(at_ps, g.n + 1)
                wait(act, z_ps, g.n)
                act.activation(a_t[:, :, 0:g.p], bank[2][:, 0:2 * P].rearrange("f (q e) -> f q e", q=2)[:, :, 0:g.p],
                               ACT.Copy).then_inc(at_sb, 1)

            def expo(g, k):
                act.wait_ge(cap_ready, g.n * 2 + k + 1)
                act.activation(expz[:, k], capped[:, k], ACT.Exp).then_inc(exp_ready, 1)

            def loga(g, k):
                act.wait_ge(exp_ready, g.n * 2 + k + 1)
                wait(act, ssp_ready, (g.n - 1) * 2 + k + 1)
                act.activation(lnz[:, k], expz[:, k], ACT.Ln, bias=half[:], scale=0.5).then_inc(ln_ready, 1)

            def keep_sum(g, q):
                act.wait_ge(sum_ps, g.n * 2 + q + 1)
                wait(act, y_ps, g.n * 2 + q - 1)
                act.activation(sum_t[:, q].rearrange("f k h e -> f (k h) e")[:, :, 0:g.p],
                               bank[6][:].rearrange("f (b e) -> f b e", b=4)[:, :, 0:g.p], ACT.Copy).then_inc(sum_sb, 1)

            def keep_y(g, q):
                act.wait_ge(y_ps, g.n * 2 + q + 1)
                wait(act, added, (g.n * R + 2 * q - 2) * 16)
                act.activation(y[q][0:g.p], bank[7][0:g.p], ACT.Copy).then_inc(y_sb, 1)

            def step(ahead, behind, last):
                if ahead is not None:
                    keep(ahead)
                if last is not None:
                    keep_y(last, 1)
                if ahead is not None:
                    expo(ahead, 0)
                    expo(ahead, 1)
                if behind is not None:
                    keep_sum(behind, 0)
                if ahead is not None:
                    loga(ahead, 0)
                    loga(ahead, 1)
                if behind is not None:
                    keep_y(behind, 0)
                    keep_sum(behind, 1)

            act.wait_ge(tab_sb, 1)
            step(group(0), None, None)
            step(group(1), group(0), None)
            for n in range(2, PEEL):
                step(group(n), group(n - 1), group(n - 2))
            with act.Fori(0, ROUNDS) as i:
                for u in range(2):
                    step(looped(i, u), looped(i, u, 1), looped(i, u, 2))
            step(group(G - 1), group(G - 2), group(G - 3))
            step(None, group(G - 1), group(G - 2))
            keep_y(group(G - 1), 1)

            def softplus2(g):
                for h in range(H):
                    act.wait_ge(cap2, g.n * H + h + 1)
                    act.activation(expz[:, h], capped[:, h], ACT.Exp).then_inc(exp2, 1)
                for h in range(H):
                    act.wait_ge(exp2, g.n * H + h + 1)
                    wait(act, ssp2_ready, (g.n - 1) * H + h + 1)
                    act.activation(lnz[:, h], expz[:, h], ACT.Ln, bias=half[:], scale=0.5).then_inc(ln2, 1)

            def norm(g):
                act.wait_ge(nmr_ready, g.n + 1)
                if not isinstance(g.n, int) or g.n >= 2:
                    act.wait_ge(stored[g.par], (g.nth - 1) * 16)
                for r in range(R):
                    last = act.activation(normed[0:g.p, g.par, r], res[0:g.p, g.par, r], ACT.Identity,
                                          bias=nmr[0:g.p, g.par, r:r + 1], scale=rstd[0:g.p, g.par, r:r + 1])
                last.then_inc(norm_ready, 1)

            softplus2(group(0))
            for n in range(1, PEEL):
                softplus2(group(n))
                norm(group(n - 1))
            with act.Fori(0, ROUNDS) as i:
                for u in range(2):
                    softplus2(looped(i, u))
                    norm(looped(i, u, 1))
            softplus2(group(G - 1))
            norm(group(G - 2))
            norm(group(G - 1))

        @block.vector
        def _(dve):
            dve.memset(rows_i[:], 0).then_inc(dve_own, 1)
            dve.memset(rows_f[:, 2], 0.0).then_inc(dve_own, 1)
            dve.memset(half[:], 0.5).then_inc(dve_own, 1)
            dve.memset(zeros[:], 0.0).then_inc(dve_own, 1)
            dve.wait_ge(dve_own, 4)
            dve.sem_inc(rows_zero, 1)
            dve.wait_ge(rows_in, 16 * 6)
            dve.tensor_copy(rows_f[:, 0:2], rows_i[:]).then_inc(rows_cast, 1)
            dve.wait_ge(made, 4)
            dve.tensor_copy(spare_f[:], spare_i[:]).then_inc(dve_own, 1)
            for k, table in enumerate((src_t, dst_t, wgt_t)):
                dve.wait_ge(tab_ps, k + 1)
                dve.tensor_copy(table[:].rearrange("p r g -> p (r g)"), bank[k][:, 0:R * G]).then_inc(dve_own, 1)
            dve.wait_ge(dve_own, 8)
            dve.tensor_scalar(to_spare[:], src_t[:], -1.0, spare_f[:, 0:1], ALU.mult, ALU.add).then_inc(dve_own, 1)
            dve.wait_ge(const_in, 16 * CONSTS)
            dve.tensor_scalar(bf1s[:], bf1[:], LOG2, None, ALU.subtract).then_inc(dve_own, 1)
            dve.tensor_scalar(bo1s[:], bo1[:], LOG2, None, ALU.subtract).then_inc(dve_own, 1)
            dve.tensor_scalar(bo2h[:], bo2h[:], 0.5, None, ALU.mult).then_inc(dve_own, 1)
            dve.wait_ge(dve_own, 12)
            dve.sem_inc(tab_sb, 1)

            def gather_ix(g):
                wait(dve, xt_ps, (g.n - 1) * 2)
                for r in range(R):
                    last = dve.tensor_copy(dst_ix[g.par][r][0:g.p], col(dst_t, r, g, g.p))
                last.then_inc(dst_ready, 1)

            def compare(g):
                dve.wait_ge(srcb_in[g.par], g.nth * 16)
                wait(dve, sum_ps, (g.n - 1) * 2)
                for r in range(R):
                    dve.tensor_scalar(same[0:g.p, g.par, r, 0:g.p], srcb[0:g.p, g.par, r:R * g.p:R], col(src_t, r, g, g.p), None,
                                      ALU.is_equal).then_inc(same_ready, 1)
                dve.wait_ge(same_ready, g.n * R + R)
                for r in range(R):
                    dve.tensor_tensor_reduce(out=junk[0:g.p, r, 0:g.p], in0=same[0:g.p, g.par, r, 0:g.p], in1=below[0:g.p, 0:g.p],
                                             scale=1.0, scalar=0.0, op0=ALU.mult, op1=ALU.add,
                                             accum_out=earlier[0:g.p, g.par, r:r + 1]).then_inc(earlier_ready, 1)
                dve.wait_ge(earlier_ready, g.n * R + R)
                dve.scalar_tensor_tensor(out=move[0:g.p], in0=earlier[0:g.p, g.par], scalar=0.0,
                                         in1=to_spare[0:g.p, :, bass.ds(g.n, 1)].squeeze(2), op0=ALU.is_gt, op1=ALU.mult).then_inc(move_ready, 1)
                dve.wait_ge(move_ready, g.n + 1)
                wait(dve, added, (g.n - 1) * R * 16)
                for r in range(R):
                    last = dve.tensor_tensor(src_ix[g.par][r][0:g.p], move[0:g.p, r:r + 1], col(src_t, r, g, g.p), ALU.add)
                last.then_inc(src_ready, 1)

            def message(g, r):
                k = r % 2
                dve.wait_ge(hw_ps, g.n * R + r + 1)
                dve.tensor_tensor(filt[0:g.p, k], bank[4 + k][0:g.p, D:2 * D], bf2b[0:g.p], ALU.add).then_inc(filt_ready, 1)
                wait(dve, sum_ps, g.n * 2 + r // 2 - 1)
                dve.wait_ge(filt_ready, g.n * R + r + 1)
                dve.scalar_tensor_tensor(out=msg[0:g.p, r], in0=filt[0:g.p, k], scalar=col(wgt_t, r, g, g.p),
                                         in1=bank[4 + k][0:g.p, 0:D], op0=ALU.mult, op1=ALU.mult).then_inc(msg_ready, 1)

            def cap(g):
                dve.wait_ge(z_ps, g.n + 1)
                for k in range(2):
                    wait(dve, exp_ready, (g.n - 1) * 2 + k + 1)
                    for h in range(H):
                        last = dve.tensor_scalar(capped[:, k, h * D:(h + 1) * D], bank[2 + k][:, h * D:(h + 1) * D],
                                                 bf1[:, h:h + 1], EXP_CAP, ALU.add, ALU.min)
                    last.then_inc(cap_ready, 1)

            def softplus(g):
                wait(dve, hw_ps, (g.n - 1) * R)
                for k in range(2):
                    dve.wait_ge(ln_ready, g.n * 2 + k + 1)
                    for h in range(H):
                        last = dve.scalar_tensor_tensor(out=ssp[:, g.par, k, h].rearrange("m q e -> m (q e)"), in0=bank[2 + k][:, h * D:(h + 1) * D],
                                                        scalar=bf1s[:, h:h + 1], in1=lnz[:, k, h * D:(h + 1) * D], op0=ALU.add, op1=ALU.max)
                    last.then_inc(ssp_ready, 1)

            def step(ahead, behind, ahead2):
                if ahead2 is not None:
                    gather_ix(ahead2)
                if behind is not None:
                    message(behind, 0)
                    message(behind, 1)
                if ahead is not None:
                    cap(ahead)
                if behind is not None:
                    message(behind, 2)
                if ahead is not None:
                    softplus(ahead)
                if behind is not None:
                    message(behind, 3)
                if ahead is not None:
                    compare(ahead)

            gather_ix(group(0))
            step(group(0), None, group(1))
            for n in range(1, PEEL):
                step(group(n), group(n - 1), group(n + 1))
            with dve.Fori(0, ROUNDS) as i:
                for u in range(2):
                    step(looped(i, u), looped(i, u, 1), looped(i, u, -1))
            step(group(G - 1), group(G - 2), None)
            step(None, group(G - 1), None)

            def cap_2(g):
                for h in range(H):
                    dve.wait_ge(mt_ps, g.n * H + h + 1)
                    wait(dve, exp2, (g.n - 1) * H + h + 1)
                    dve.tensor_scalar(capped[:, h], bank[2 * g.par + h][:], bo1[:, h:h + 1], EXP_CAP,
                                      ALU.add, ALU.min).then_inc(cap2, 1)

            def softplus_2(g):
                wait(dve, o_ps, (g.n - 1) * 2)
                for h in range(H):
                    dve.wait_ge(ln2, g.n * H + h + 1)
                    dve.scalar_tensor_tensor(out=ssp2[:, g.par, h].rearrange("m r n -> m (r n)"), in0=bank[2 * g.par + h][:],
                                             scalar=bo1s[:, h:h + 1], in1=lnz[:, h], op0=ALU.add, op1=ALU.max).then_inc(ssp2_ready, 1)

            def residual(g):
                dve.wait_ge(xb_ready, g.n + 1)
                wait(dve, norm_ready, g.n - 1)
                for q in range(2):
                    dve.wait_ge(o_ps, g.n * 2 + q + 1)
                    dve.scalar_tensor_tensor(out=res[0:g.p, g.par, 2 * q:2 * q + 2].rearrange("p k d -> p (k d)"),
                                             in0=xb[0:g.p, g.par, 2 * q:2 * q + 2].rearrange("p k d -> p (k d)"), scalar=2.0,
                                             in1=bank[4 + 2 * g.par + q][0:g.p], op0=ALU.mult, op1=ALU.add).then_inc(res_ready, 1)
                dve.wait_ge(res_ready, g.n * 2 + 2)
                for r in range(R):
                    last = dve.bn_stats(stats[0:g.p, g.par, r], res[0:g.p, g.par, r])
                last.then_inc(stat_ready, 1)
                dve.wait_ge(stat_ready, g.n + 1)
                dve.sem_inc(dve_step, 1)
                for r in range(R):
                    last = dve.bn_aggr(mv[0:g.p, g.par, r], stats[0:g.p, g.par, r])
                last.then_inc(mv_ready, 1)
                dve.wait_ge(mv_ready, g.n + 1)
                dve.tensor_scalar(veps[0:g.p, g.par], mv[0:g.p, g.par, :, 1], EPS, None, ALU.add).then_inc(veps_ready, 1)

            def factors(g):
                dve.wait_ge(rstd_ready, g.n + 1)
                dve.scalar_tensor_tensor(out=nmr[0:g.p, g.par], in0=mv[0:g.p, g.par, :, 0], scalar=-1.0, in1=rstd[0:g.p, g.par],
                                         op0=ALU.mult, op1=ALU.mult).then_inc(nmr_ready, 1)

            def step2(ahead, behind):
                if ahead is not None:
                    cap_2(ahead)
                if behind is not None:
                    residual(behind)
                if ahead is not None:
                    softplus_2(ahead)
                if behind is not None:
                    factors(behind)

            step2(group(0), None)
            for n in range(1, PEEL):
                step2(group(n), group(n - 1))
            with dve.Fori(0, ROUNDS) as i:
                for u in range(2):
                    step2(looped(i, u), looped(i, u, 1))
            step2(group(G - 1), group(G - 2))
            step2(None, group(G - 1))


_OUT = (50000, 256)


def kernel(**inputs):
    import numpy as np
    import concourse.bacc as bacc
    from concourse.bass_utils import run_bass_kernel_spmd

    nc = bacc.Bacc("TRN2", target_bir_lowering=False, num_devices=1)
    arrays, t = {}, {}
    for name, value in inputs.items():
        a = np.ascontiguousarray(value)
        arrays[f"in_{name}"] = a
        t[name] = nc.dram_tensor(f"in_{name}", a.shape, mybir.dt.from_np(a.dtype), kind="ExternalInput").ap()
    out = nc.dram_tensor("out_0", _OUT, F32, kind="ExternalOutput").ap()
    build(nc, t, out)
    return run_bass_kernel_spmd(nc, [arrays], core_ids=[0]).results[0]["out_0"]
```

```python
from contextlib import ExitStack

import concourse.bass as bass
from concourse import mybir

ALU = mybir.AluOpType
ACT = mybir.ActivationFunctionType
F32 = mybir.dt.float32
F32R = mybir.dt.float32r
I32 = mybir.dt.int32

P = 128
R = 4
LOG2 = 0.6931471805599453
EXP_CAP = 40.0
EPS = 1e-5


class Group:

    def __init__(self, number, parity, nth, rows):
        self.n, self.par, self.nth, self.rows = number, parity, nth, rows
        self.p = rows // R


def wait(eng, sem, value):
    if isinstance(value, int) and value <= 0:
        return
    eng.wait_ge(sem, value)


def build(nc, t, out):
    N, D = t["x"].shape
    E = t["src"].shape[0]
    A = t["edge_attr_64"].shape[1]
    H = D // P
    ROWS = R * P
    assert D == 2 * P and 2 * A == P and E == N and E % R == 0
    G = -(-E // ROWS)
    TAIL = E - (G - 1) * ROWS

    def group(n):
        return Group(n, n % 2, n // 2 + 1, ROWS if n < G - 1 else TAIL)

    def run(eng, *stages, peel=0):
        lags = [lag for _, lag in stages]
        first = max(max(lags) + 2, peel)
        first += (G - 1 - first) % 2
        rounds = (G - 1 - first) // 2

        def straight(steps):
            for s in steps:
                for stage, lag in stages:
                    if 0 <= s - lag < G:
                        stage(group(s - lag))

        straight(range(first))
        with eng.Fori(0, rounds) as i:
            for u in range(2):
                for stage, lag in stages:
                    k = first + u - lag
                    stage(Group(i * 2 + k, k % 2, i + (k // 2 + 1), ROWS))
        straight(range(first + 2 * rounds, G + max(lags)))

    acc = nc.dram_tensor("acc", [N + P, D], F32, kind="Internal").ap()

    with ExitStack() as ctx:
        def sb(name, shape, dt=F32):
            return ctx.enter_context(nc.sbuf_tensor(name, shape, dt))

        def sem(name):
            return ctx.enter_context(nc.semaphore(name))

        bank = [ctx.enter_context(nc.psum_tensor(f"bank{i}", [P, 512], F32)) for i in range(8)]

        ident = sb("ident", [P, P])
        below = sb("below", [P, P])
        ones = sb("ones", [2, P])
        ones_r = sb("ones_r", [2, P], F32R)
        w_in, wf2, wo1, wo2 = (sb(n, [P, H, D]) for n in ("w_in", "wf2", "wo1", "wo2"))
        w_in_h, w_in_l, wf2_h, wf2_l, wo1_h, wo1_l = (
            sb(n, [P, H, D], F32R) for n in ("w_in_h", "w_in_l", "wf2_h", "wf2_l", "wo1_h", "wo1_l"))
        wf1 = sb("wf1", [P, D])
        wf1_h = sb("wf1_h", [P, D], F32R)
        wf1_hl = sb("wf1_hl", [P, D], F32R)
        bf1, bf2, bo1 = (sb(n, [P, H]) for n in ("bf1", "bf2", "bo1"))
        neg_bf1 = sb("neg_bf1", [P, H])
        bo1_less = sb("bo1_less", [P, H])
        bf1_two = sb("bf1_two", [P, H, 2])
        bias_w = sb("bias_w", [P, H])
        bo2 = sb("bo2", [2, D])
        bo2_h, bo2_l = sb("bo2_h", [2, D], F32R), sb("bo2_l", [2, D], F32R)
        bo2_hl = sb("bo2_hl", [2, D], F32R)
        rows_i = sb("rows_i", [P, ROWS], I32)
        rows_f = sb("rows_f", [P, 2, ROWS])
        src_t, wgt_t = (sb(n, [P, R, G]) for n in ("src_t", "wgt_t"))
        spare_i = sb("spare_i", [P, 1], I32)
        spare_f = sb("spare_f", [P, 1])
        to_spare = sb("to_spare", [P, R, G])
        half = sb("half", [P, 1])
        neg_half = sb("neg_half", [P, R])
        CLEAR = 10
        zeros = sb("zeros", [P, CLEAR * D])

        attr = sb("attr", [P, 2, R, 2, A])
        srcb = sb("srcb", [P, 2, ROWS], I32)
        xg = [[sb(f"xg{u}{r}", [P, D]) for r in range(R)] for u in range(2)]
        dst_ix = [sb(f"dst_ix{u}", [P, R], I32) for u in range(2)]
        src_ix = [[sb(f"src_ix{u}{r}", [P, 1], I32) for r in range(R)] for u in range(2)]
        x_h, x_l = (sb(n, [P, 2, H, R, P], F32R) for n in ("x_h", "x_l"))
        a_h, a_l = (sb(n, [P, R, P], F32R) for n in ("a_h", "a_l"))
        absz, expz, lnz, ssp = (sb(n, [P, H, 512]) for n in ("absz", "expz", "lnz", "ssp"))
        ssp_h, ssp_l = (sb(n, [P, 2, H, R, P], F32R) for n in ("ssp_h", "ssp_l"))
        same = sb("same", [P, 2, R, P], F32R)
        junk = sb("junk", [P, R, P])
        earlier = sb("earlier", [P, 2, R])
        move = sb("move", [P, R])
        h_sb, msg = (sb(n, [P, H, 512]) for n in ("h_sb", "msg"))
        msg_h, msg_l = (sb(n, [P, H, R, P], F32R) for n in ("msg_h", "msg_l"))
        m_h, m_l = (sb(n, [P, R, D], F32R) for n in ("m_h", "m_l"))
        y = sb("y", [P, 2, R, D])

        m_in, x_in, res = (sb(n, [P, 2, R, D]) for n in ("m_in", "x_in", "res"))
        capped = absz
        normed = y
        ssp2 = sb("ssp2", [P, 2, H, R, P])
        squares = msg
        total, neg_mean, square, veps, rstd = (sb(n, [P, 2, R]) for n in ("total", "neg_mean", "square", "veps", "rstd"))

        dve_own = sem("dve_own")
        const_in = sem("const_in")
        rows_in = sem("rows_in")
        rows_zero = sem("rows_zero")
        zeros_made = sem("zeros_made")
        rows_cast = sem("rows_cast")
        made = sem("made")
        cleared = sem("cleared")
        tab_ps = sem("tab_ps")
        tab_sb = sem("tab_sb")
        two_made = sem("two_made")
        bias_ps = sem("bias_ps")
        const_made = sem("const_made")
        attr_in = [sem(f"attr_in{u}") for u in range(2)]
        srcb_in = [sem(f"srcb_in{u}") for u in range(2)]
        xg_in = [[sem(f"xg_in{u}{r}") for r in range(R)] for u in range(2)]
        added = sem("added")
        dst_in = [sem(f"dst_in{u}") for u in range(2)]
        src_ready = sem("src_ready")
        same_ready = sem("same_ready")
        earlier_ready, move_ready = sem("earlier_ready"), sem("move_ready")
        xt_ps = sem("xt_ps")
        xh_sb, xl_sb = sem("xh_sb"), sem("xl_sb")
        at_ps = sem("at_ps")
        ah_sb, al_sb = sem("ah_sb"), sem("al_sb")
        z_ps = sem("z_ps")
        abs_sb, exp_sb, ln_sb, ssp_sb, ssph_sb, sspl_sb = (
            sem(n) for n in ("abs_sb", "exp_sb", "ln_sb", "ssp_sb", "ssph_sb", "sspl_sb"))
        h_ps, w_ps = sem("h_ps"), sem("w_ps")
        h_kept = sem("h_kept")
        msg_sb = sem("msg_sb")
        msgh_sb, msgl_sb = sem("msgh_sb"), sem("msgl_sb")
        m_ps = sem("m_ps")
        mh_sb, ml_sb = sem("mh_sb"), sem("ml_sb")
        y_ps, y_sb = sem("y_ps"), sem("y_sb")
        pool_step, sp_step = sem("pool_step"), sem("sp_step")
        m_got = [sem(f"m_got{u}") for u in range(2)]
        x_got = [sem(f"x_got{u}") for u in range(2)]
        mt_ps = sem("mt_ps")
        cap2, exp2, ln2, ssp2_sb = (sem(n) for n in ("cap2", "exp2", "ln2", "ssp2_sb"))
        o_ps = sem("o_ps")
        res_sb, mean_sb = sem("res_sb"), sem("mean_sb")
        square_sb = sem("square_sb")
        veps_sb = sem("veps_sb")
        rstd_sb, norm_sb = sem("rstd_sb"), sem("norm_sb")
        stored = [sem(f"stored{u}") for u in range(2)]

        block = ctx.enter_context(nc.Block())

        CONSTS = 13
        CLEARS = N // P // CLEAR
        CLEARS_A_STEP = 8
        assert N // P % CLEAR == 0

        def rows_of(ap, g):
            return ap[bass.ds(g.n * ROWS, g.rows)]

        def col(table, r, g):
            return table[0:g.p, r, bass.ds(g.n, 1)]

        @block.sync
        def _(sp):
            sp.wait_ge(rows_zero, 1)
            flat = t["edge_weight1"].rearrange("e a -> (e a)")
            for dest, ap in ((rows_i, t["src"]), (rows_f[:, 1], flat)):
                sp.dma_start(dest[0:G - 1, :], ap[0:(G - 1) * ROWS].rearrange("(g e) -> g e", e=ROWS)).then_inc(rows_in, 16)
                sp.dma_start(dest[G - 1:G, 0:TAIL], ap[(G - 1) * ROWS:E].rearrange("(g e) -> g e", e=TAIL)).then_inc(rows_in, 16)
            for k in range(2):
                sp.dma_start(wf1[k * A:(k + 1) * A, :], t["L0_gnn_Wf1"]).then_inc(const_in, 16)
            for w, name in ((w_in, "L0_gnn_W_in2f"), (wf2, "L0_gnn_Wf2"), (wo1, "L0_gnn_Wo1"), (wo2, "L0_gnn_Wo2")):
                sp.dma_start(w[:], t[name].rearrange("(h p) n -> p h n", p=P)).then_inc(const_in, 16)
            for b, name in ((bf1, "L0_gnn_bf1"), (bf2, "L0_gnn_bf2"), (bo1, "L0_gnn_bo1")):
                for h in range(H):
                    sp.dma_start(b[:, h:h + 1], t[name][h * P:(h + 1) * P].rearrange("(p a) -> p a", a=1)).then_inc(const_in, 16)
            sp.dma_start(bo2[:], t["L0_gnn_bo2"].partition_broadcast(2)).then_inc(const_in, 16)

            def load_dst(g):
                wait(sp, xt_ps, (g.n - 1) * 2)
                sp.sem_inc(sp_step, 1)
                sp.dma_start(dst_ix[g.par][0:g.p], rows_of(t["dst"], g).rearrange("(p r) -> p r", r=R)).then_inc(dst_in[g.par], 16)

            def load_attr(g):
                wait(sp, at_ps, g.n - 1)
                sp.sem_inc(sp_step, 1)
                for k in range(2):
                    sp.dma_start(attr[0:g.p, g.par, :, k, :], rows_of(t["edge_attr_64"], g).rearrange("(p r) a -> p r a", r=R)).then_inc(attr_in[g.par], 16)

            def load_src(g):
                wait(sp, same_ready, (g.n - 1) * R)
                sp.sem_inc(sp_step, 1)
                sp.dma_start(srcb[:, g.par, 0:g.rows], rows_of(t["src"], g).partition_broadcast(P)).then_inc(srcb_in[g.par], 16)

            def clear(g):
                if isinstance(g.n, int) and g.n * CLEARS_A_STEP <= CLEARS:
                    for c in range(g.n * CLEARS_A_STEP, min((g.n + 1) * CLEARS_A_STEP, CLEARS)):
                        sp.dma_start(acc[c * CLEAR * P:(c + 1) * CLEAR * P, :].rearrange("(p k) d -> p (k d)", k=CLEAR), zeros[:]).then_inc(cleared, 16)
                    if (g.n + 1) * CLEARS_A_STEP > CLEARS:
                        rest = N + P - CLEARS * CLEAR * P
                        sp.dma_start(acc[CLEARS * CLEAR * P:N + P, :].rearrange("(p k) d -> p (k d)", k=2), zeros[0:rest // 2, 0:2 * D]).then_inc(cleared, 16)

            sp.wait_ge(zeros_made, 1)
            run(sp, (load_dst, 0), (load_attr, 0), (load_src, 2), (clear, 0), peel=CLEARS // CLEARS_A_STEP + 1)

            sp.wait_ge(added, 16 * R * G)

            def fetch_m(g):
                wait(sp, mt_ps, (g.n - 1) * H)
                sp.sem_inc(sp_step, 1)
                sp.dma_start(m_in[0:g.p, g.par].rearrange("p r d -> p (r d)"), rows_of(acc, g).rearrange("(p r) d -> p (r d)", r=R)).then_inc(m_got[g.par], 16)

            def fetch_x(g):
                wait(sp, res_sb, g.n - 1)
                sp.sem_inc(sp_step, 1)
                sp.dma_start(x_in[0:g.p, g.par].rearrange("p r d -> p (r d)"), rows_of(t["x"], g).rearrange("(p r) d -> p (r d)", r=R)).then_inc(x_got[g.par], 16)

            def store(g):
                wait(sp, norm_sb, g.n + 1)
                sp.sem_inc(sp_step, 1)
                sp.dma_start(rows_of(out, g).rearrange("(p r) d -> p (r d)", r=R), normed[0:g.p, g.par].rearrange("p r d -> p (r d)")).then_inc(stored[g.par], 16)

            run(sp, (fetch_m, 0), (fetch_x, 1), (store, 5))
            for u in range(2):
                sp.wait_ge(stored[u], 16 * len(range(u, G, 2)))

        @block.gpsimd
        def _(pool):
            pool.memset(ident[:], 0.0).then_inc(pool_step, 1)
            pool.memset(below[:], 1.0).then_inc(pool_step, 1)
            pool.memset(neg_half[:], -0.5).then_inc(made, 1)
            pool.memset(half[:], 0.5).then_inc(made, 1)
            pool.memset(ones[:], 1.0).then_inc(made, 1)
            pool.iota(spare_i[:], [[0, 1]], base=N, channel_multiplier=1).then_inc(made, 1)
            pool.wait_ge(pool_step, 2)
            pool.affine_select(out=ident[:], in_=ident[:], compare_op=ALU.not_equal, fill=1.0, base=0,
                               pattern=[[-1, P]], channel_multiplier=1).then_inc(made, 1)
            pool.affine_select(out=below[:], in_=below[:], compare_op=ALU.is_gt, fill=0.0, base=0,
                               pattern=[[-1, P]], channel_multiplier=1).then_inc(made, 1)
            pool.memset(zeros[:], 0.0).then_inc(zeros_made, 1)

            def gather(r):
                def stage(g):
                    pool.wait_ge(dst_in[g.par], g.nth * 16)
                    wait(pool, xt_ps, (g.n - 1) * 2)
                    pool.sem_inc(pool_step, 1)
                    pool.indirect_dma_start(xg[g.par][r][0:g.p, :], None, t["x"],
                                            bass.IndirectOffsetOnAxis(ap=dst_ix[g.par][0:g.p, r:r + 1], axis=0)).then_inc(xg_in[g.par][r], 16)
                return stage

            def scatter(r):
                def stage(g):
                    if isinstance(g.n, int) and g.n == 0 and r == 0:
                        pool.wait_ge(cleared, 16 * (CLEARS + 1))
                    wait(pool, src_ready, g.n + 1)
                    wait(pool, y_sb, g.n * 2 + r // 2 + 1)
                    wait(pool, added, (g.n * R + r) * 16)
                    pool.sem_inc(pool_step, 1)
                    pool.indirect_dma_start(acc, bass.IndirectOffsetOnAxis(ap=src_ix[g.par][r][0:g.p, :], axis=0),
                                            y[0:g.p, g.par, r], None, compute_op=ALU.add).then_inc(added, 16)
                return stage

            run(pool, (scatter(2), 6), (gather(0), 0), (scatter(3), 6), (gather(1), 0), (scatter(0), 5), (gather(2), 0),
                (scatter(1), 5), (gather(3), 0))

            def norm(g):
                pool.wait_ge(veps_sb, g.n + 1)
                pool.tensor_tensor(rstd[0:g.p, g.par], veps[0:g.p, g.par], neg_half[0:g.p], ALU.pow).then_inc(rstd_sb, 1)
                pool.wait_ge(rstd_sb, g.n + 1)
                if not isinstance(g.n, int) or g.n >= 2:
                    pool.wait_ge(stored[g.par], (g.nth - 1) * 16)
                pool.sem_inc(pool_step, 1)
                for r in range(R):
                    last = pool.tensor_scalar(normed[0:g.p, g.par, r], res[0:g.p, g.par, r], neg_mean[0:g.p, g.par, r:r + 1],
                                              rstd[0:g.p, g.par, r:r + 1], ALU.add, ALU.mult)
                last.then_inc(norm_sb, 1)

            run(pool, (norm, 0))

        @block.tensor
        def _(pe):
            pe.wait_ge(made, 6)
            pe.wait_ge(rows_cast, 1)
            for k in range(2):
                if k == 1:
                    pe.wait_ge(rows_in, 16 * 4)
                for r in range(R):
                    last = pe.transpose(bank[k][:, r * G:(r + 1) * G], rows_f[0:G, k, r::R], ident[0:G, 0:G])
                last.then_inc(tab_ps, 1)
            pe.wait_ge(two_made, 1)
            for m in range(H):
                for k in range(H):
                    last = pe.matmul(bank[3][:, 2 * m:2 * m + 2], wf2[:, k, m * P:(m + 1) * P], bf1_two[:, k], start=k == 0, stop=k == H - 1)
            last.then_inc(bias_ps, 1)
            pe.wait_ge(tab_sb, 1)

            def three(o, stat_h, stat_l, mov_h, mov_l):
                terms = [ab for sh, sl, mh, ml in zip(stat_h, stat_l, mov_h, mov_l) for ab in ((sh, mh), (sh, ml), (sl, mh))]
                for n, (a, b) in enumerate(terms):
                    last = pe.matmul(o, a, b, start=n == 0, stop=n == len(terms) - 1)
                return last

            def turn_x(q):
                def stage(g):
                    for k in range(2):
                        pe.wait_ge(xg_in[g.par][2 * q + k], g.nth * 16)
                    wait(pe, xl_sb, (g.n - 1) * 2 + q + 1)
                    for h in range(H):
                        for k in range(2):
                            c = (h * 2 + k) * P
                            last = pe.transpose(bank[q][:, c:c + g.p], xg[g.par][2 * q + k][0:g.p, h * P:(h + 1) * P], ident[0:g.p, 0:g.p])
                    last.then_inc(xt_ps, 1)
                return stage

            def turn_a(g):
                pe.wait_ge(attr_in[g.par], g.nth * 32)
                wait(pe, ssp_sb, g.n * H)
                for r in range(R):
                    last = pe.transpose(bank[2][:, r * P:r * P + g.p],
                                        attr[0:g.p, g.par, r].rearrange("e k a -> e (k a)"), ident[0:g.p, 0:g.p])
                last.then_inc(at_ps, 1)

            def filter1(g):
                pe.wait_ge(al_sb, g.n + 1)
                wait(pe, ssp_sb, g.n * H)
                for h in range(H):
                    o = bank[2 + h][:].rearrange("m (r e) -> m r e", r=R)[:, :, 0:g.p]
                    pe.matmul(o, wf1_hl[:, h * P:(h + 1) * P], a_h[:, :, 0:g.p], start=True, stop=False)
                    last = pe.matmul(o, wf1_hl[:, h * P:(h + 1) * P], a_l[:, :, 0:g.p], start=False, stop=True)
                last.then_inc(z_ps, 1)

            def transposed(m, psum, w_h, w_l, in_h, in_l):
                cols = slice(m * P, (m + 1) * P)
                return three(psum, [w_h[:, k, cols] for k in range(H)], [w_l[:, k, cols] for k in range(H)], in_h, in_l)

            def h_of(m):
                def stage(g):
                    if m == 0:
                        pe.wait_ge(xl_sb, g.n * 2 + 2)
                    wait(pe, h_kept, g.n * H + m)
                    transposed(m, bank[4][:].rearrange("f (r e) -> f r e", r=R)[:, :, 0:g.p], w_in_h, w_in_l,
                               [x_h[:, g.par, k, :, 0:g.p] for k in range(H)], [x_l[:, g.par, k, :, 0:g.p] for k in range(H)]).then_inc(h_ps, 1)
                return stage

            def w_of(m):
                def stage(g):
                    if m == 0:
                        pe.wait_ge(sspl_sb, g.n * H + H)
                    wait(pe, msg_sb, g.n * H + m)
                    transposed(m, bank[5][:].rearrange("f (r e) -> f r e", r=R)[:, :, 0:g.p], wf2_h, wf2_l,
                               [ssp_h[:, g.par, k, :, 0:g.p] for k in range(H)], [ssp_l[:, g.par, k, :, 0:g.p] for k in range(H)]).then_inc(w_ps, 1)
                return stage

            def out1(q):
                def stage(g):
                    if q == 0:
                        pe.wait_ge(msgl_sb, g.n * H + H)
                    wait(pe, ml_sb, g.n * R + 2 * q)
                    for k in range(2):
                        last = three(bank[6][0:g.p, k * D:(k + 1) * D],
                                     [msg_h[:, h, 2 * q + k, 0:g.p] for h in range(H)], [msg_l[:, h, 2 * q + k, 0:g.p] for h in range(H)],
                                     [wo1_h[:, h] for h in range(H)], [wo1_l[:, h] for h in range(H)])
                    last.then_inc(m_ps, 1)
                return stage

            def summed(q):
                def stage(g):
                    pe.wait_ge(ml_sb, g.n * R + 2 * q + 2)
                    if q == 0:
                        pe.wait_ge(same_ready, g.n * R + R)
                    wait(pe, y_sb, g.n * 2 + q)
                    for k in range(2):
                        r, o = 2 * q + k, bank[7][0:g.p, k * D:(k + 1) * D]
                        pe.matmul(o, same[0:g.p, g.par, r, 0:g.p], m_h[0:g.p, r], start=True, stop=False)
                        last = pe.matmul(o, same[0:g.p, g.par, r, 0:g.p], m_l[0:g.p, r], start=False, stop=True)
                    last.then_inc(y_ps, 1)
                return stage

            pe.wait_ge(const_made, 1)
            run(pe, (h_of(0), 2), (turn_x(1), 1), (summed(1), 4), (out1(0), 3), (filter1, 1), (w_of(0), 2), (h_of(1), 2),
                (summed(0), 3), (out1(1), 3), (w_of(1), 2), (turn_x(0), 0), (turn_a, 0))

            def turn2(g):
                pe.wait_ge(m_got[g.par], g.nth * 16)
                wait(pe, ssp2_sb, (g.n - 1) * H)
                for h in range(H):
                    for r in range(R):
                        last = pe.transpose(bank[2 * g.par + h][:, r * P:r * P + g.p], m_in[0:g.p, g.par, r, h * P:(h + 1) * P], ident[0:g.p, 0:g.p])
                    last.then_inc(mt_ps, 1)

            def out2(g):
                pe.wait_ge(ssp2_sb, g.n * H + H)
                wait(pe, res_sb, g.n - 1)
                for q in range(2):
                    for k in range(2):
                        o = bank[4 + 2 * g.par + q][0:g.p, k * D:(k + 1) * D]
                        for h in range(H):
                            pe.matmul(o, ssp2[:, g.par, h, 2 * q + k, 0:g.p], wo2[:, h, :], start=h == 0, stop=False)
                        last = pe.matmul(o, ones_r[:, 0:g.p], bo2_hl[:], start=False, stop=True)
                    last.then_inc(o_ps, 1)

            run(pe, (turn2, 0), (out2, 1))

        @block.scalar
        def _(act):
            act.preload_act_table_set("natural_log_exp_and_others")

            def high(out_, in_, done):
                act.activation(out_, in_, ACT.Copy).then_inc(done, 1)

            def x_high(q):
                def stage(g):
                    act.wait_ge(xt_ps, g.n * 2 + q + 1)
                    wait(act, h_ps, (g.n - 1) * H)
                    high(x_h[:, g.par, :, 2 * q:2 * q + 2, 0:g.p], bank[q][:].rearrange("f (h k e) -> f h k e", h=H, k=2)[:, :, :, 0:g.p], xh_sb)
                return stage

            def a_high(g):
                act.wait_ge(at_ps, g.n + 1)
                wait(act, z_ps, g.n)
                high(a_h[:, :, 0:g.p], bank[2][:].rearrange("f (r e) -> f r e", r=R)[:, :, 0:g.p], ah_sb)

            def absolute(h):
                def stage(g):
                    act.wait_ge(z_ps, g.n + 1)
                    act.activation(absz[:, h], bank[2 + h][:], ACT.Abs, bias=bf1[:, h:h + 1]).then_inc(abs_sb, 1)
                return stage

            def expo(h):
                def stage(g):
                    act.wait_ge(abs_sb, g.n * H + h + 1)
                    act.activation(expz[:, h], absz[:, h], ACT.Exp, scale=-1.0).then_inc(exp_sb, 1)
                return stage

            def loga(h):
                def stage(g):
                    act.wait_ge(exp_sb, g.n * H + h + 1)
                    wait(act, ssp_sb, (g.n - 1) * H + h + 1)
                    act.activation(lnz[:, h], expz[:, h], ACT.Ln, bias=half[:], scale=0.5).then_inc(ln_sb, 1)
                return stage

            def ssp_high(h):
                def stage(g):
                    act.wait_ge(ssp_sb, g.n * H + h + 1)
                    wait(act, w_ps, (g.n - 1) * H)
                    high(ssp_h[:, g.par, h], ssp[:, h].rearrange("m (r e) -> m r e", r=R), ssph_sb)
                return stage

            def keep_h(m):
                def stage(g):
                    act.wait_ge(h_ps, g.n * H + m + 1)
                    wait(act, msg_sb, (g.n - 1) * H + m + 1)
                    act.activation(h_sb[:, m], bank[4][:], ACT.Copy).then_inc(h_kept, 1)
                return stage

            def msg_high(m):
                def stage(g):
                    act.wait_ge(msg_sb, g.n * H + m + 1)
                    wait(act, m_ps, g.n * 2)
                    high(msg_h[:, m], msg[:, m].rearrange("f (r e) -> f r e", r=R), msgh_sb)
                return stage

            def m_high(q):
                def stage(g):
                    act.wait_ge(m_ps, g.n * 2 + q + 1)
                    wait(act, y_ps, (g.n - 1) * 2 + q + 1)
                    for k in range(2):
                        r = 2 * q + k
                        act.activation(m_h[0:g.p, r], bank[6][0:g.p, k * D:(k + 1) * D], ACT.Copy, scale=col(wgt_t, r, g)).then_inc(mh_sb, 1)
                return stage

            def keep_y(q):
                def stage(g):
                    act.wait_ge(y_ps, g.n * 2 + q + 1)
                    wait(act, added, ((g.n - 1) * R + 2 * q - 2) * 16)
                    act.activation(y[0:g.p, g.par, 2 * q:2 * q + 2].rearrange("e k d -> e (k d)"), bank[7][0:g.p], ACT.Copy).then_inc(y_sb, 1)
                return stage

            act.wait_ge(const_made, 1)
            run(act, (msg_high(1), 2), (a_high, 0), (ssp_high(1), 1), (x_high(0), 0), (keep_y(1), 3), (keep_h(0), 1),
                (x_high(1), 0), (m_high(0), 2), (absolute(0), 0), (absolute(1), 0), (expo(0), 0), (expo(1), 0), (loga(0), 0),
                (loga(1), 0), (keep_y(0), 2), (msg_high(0), 1), (keep_h(1), 1), (m_high(1), 2), (ssp_high(0), 0))

            def softplus2(g):
                for h in range(H):
                    act.wait_ge(cap2, g.n * H + h + 1)
                    act.activation(expz[:, h], capped[:, h], ACT.Exp).then_inc(exp2, 1)
                for h in range(H):
                    act.wait_ge(exp2, g.n * H + h + 1)
                    wait(act, ssp2_sb, (g.n - 1) * H + h + 1)
                    act.activation(lnz[:, h], expz[:, h], ACT.Ln, bias=half[:], scale=0.5).then_inc(ln2, 1)

            def deviation(g):
                act.wait_ge(mean_sb, g.n + 1)
                wait(act, veps_sb, g.n - 1)
                for r in range(R):
                    last = act.activation(squares[0:g.p, r // 2, r % 2 * D:(r % 2 + 1) * D], res[0:g.p, g.par, r], ACT.Square,
                                          bias=neg_mean[0:g.p, g.par, r:r + 1], accum_out=square[0:g.p, g.par, r:r + 1])
                last.then_inc(square_sb, 1)

            run(act, (softplus2, 0), (deviation, 2))

        @block.vector
        def _(dve):
            dve.memset(rows_i[:], 0).then_inc(dve_own, 1)
            dve.memset(rows_f[:, 1], 0.0).then_inc(dve_own, 1)
            dve.wait_ge(dve_own, 2)
            dve.sem_inc(rows_zero, 1)
            dve.wait_ge(rows_in, 16 * 4)
            dve.tensor_copy(rows_f[:, 0], rows_i[:]).then_inc(rows_cast, 1)
            dve.wait_ge(made, 6)
            dve.tensor_copy(spare_f[:], spare_i[:]).then_inc(dve_own, 1)
            for k, table in enumerate((src_t, wgt_t)):
                dve.wait_ge(tab_ps, k + 1)
                dve.tensor_copy(table[:].rearrange("p r g -> p (r g)"), bank[k][:, 0:R * G]).then_inc(dve_own, 1)
            dve.wait_ge(dve_own, 5)
            dve.tensor_scalar(to_spare[:], src_t[:], -1.0, spare_f[:, 0:1], ALU.mult, ALU.add).then_inc(tab_sb, 1)

            def low(out_, whole, high, done, count=1):
                dve.tensor_tensor(out_, whole, high.bitcast(F32), ALU.subtract).then_inc(done, count)

            dve.wait_ge(const_in, 16 * CONSTS)
            for k in range(2):
                dve.tensor_copy(bf1_two[:, :, k], bf1[:]).then_inc(dve_own, 1)
            dve.wait_ge(dve_own, 7)
            dve.sem_inc(two_made, 1)
            for w, wh in ((w_in, w_in_h), (wf2, wf2_h), (wo1, wo1_h), (wf1, wf1_h), (bo2, bo2_h)):
                dve.tensor_copy(wh[:], w[:]).then_inc(dve_own, 1)
            dve.tensor_copy(wf1_hl[0:A], wf1[0:A]).then_inc(dve_own, 1)
            dve.tensor_copy(ones_r[:], ones[:]).then_inc(dve_own, 1)
            dve.tensor_scalar(neg_bf1[:], bf1[:], -1.0, None, ALU.mult).then_inc(dve_own, 1)
            dve.tensor_scalar(bo1_less[:], bo1[:], LOG2, None, ALU.subtract).then_inc(dve_own, 1)
            dve.wait_ge(dve_own, 16)
            for w, wh, wl in ((w_in, w_in_h, w_in_l), (wf2, wf2_h, wf2_l), (wo1, wo1_h, wo1_l), (bo2, bo2_h, bo2_l)):
                low(wl[:], w[:], wh[:], dve_own)
            low(wf1_hl[A:P], wf1[A:P], wf1_h[A:P], dve_own)
            dve.wait_ge(bias_ps, 1)
            dve.tensor_tensor(bias_w[:], bf2[:], bank[3][:, 0:2 * H:2], ALU.add).then_inc(dve_own, 1)
            dve.wait_ge(dve_own, 22)
            dve.tensor_scalar(bo2[:], bo2_l[:].bitcast(F32), ident[0:2, 1:2], None, ALU.mult).then_inc(dve_own, 1)
            dve.wait_ge(dve_own, 23)
            dve.scalar_tensor_tensor(out=bo2_hl[:], in0=bo2_h[:].bitcast(F32), scalar=ident[0:2, 0:1], in1=bo2[:],
                                     op0=ALU.mult, op1=ALU.add).then_inc(const_made, 1)

            def x_low(q):
                def stage(g):
                    dve.wait_ge(xh_sb, g.n * 2 + q + 1)
                    wait(dve, h_ps, (g.n - 1) * H)
                    low(x_l[:, g.par, :, 2 * q:2 * q + 2, 0:g.p], bank[q][:].rearrange("f (h k e) -> f h k e", h=H, k=2)[:, :, :, 0:g.p],
                        x_h[:, g.par, :, 2 * q:2 * q + 2, 0:g.p], xl_sb)
                return stage

            def a_low(g):
                dve.wait_ge(ah_sb, g.n + 1)
                wait(dve, z_ps, g.n)
                low(a_l[:, :, 0:g.p], bank[2][:].rearrange("f (r e) -> f r e", r=R)[:, :, 0:g.p], a_h[:, :, 0:g.p], al_sb)

            def compare(g):
                dve.wait_ge(srcb_in[g.par], g.nth * 16)
                wait(dve, y_ps, (g.n - 1) * 2)
                for r in range(R):
                    dve.tensor_scalar(same[0:g.p, g.par, r, 0:g.p], srcb[0:g.p, g.par, r:R * g.p:R], col(src_t, r, g), None,
                                      ALU.is_equal).then_inc(same_ready, 1)
                dve.wait_ge(same_ready, g.n * R + R)
                for r in range(R):
                    dve.tensor_tensor_reduce(out=junk[0:g.p, r, 0:g.p], in0=same[0:g.p, g.par, r, 0:g.p].bitcast(F32), in1=below[0:g.p, 0:g.p],
                                             scale=1.0, scalar=0.0, op0=ALU.mult, op1=ALU.add,
                                             accum_out=earlier[0:g.p, g.par, r:r + 1]).then_inc(earlier_ready, 1)

            def target(g):
                dve.wait_ge(earlier_ready, g.n * R + R)
                dve.scalar_tensor_tensor(out=move[0:g.p], in0=earlier[0:g.p, g.par], scalar=0.0,
                                         in1=to_spare[0:g.p, :, bass.ds(g.n, 1)].squeeze(2), op0=ALU.is_gt, op1=ALU.mult).then_inc(move_ready, 1)
                dve.wait_ge(move_ready, g.n + 1)
                wait(dve, added, (g.n - 1) * R * 16)
                for r in range(R):
                    last = dve.tensor_tensor(src_ix[g.par][r][0:g.p], move[0:g.p, r:r + 1], col(src_t, r, g), ALU.add)
                last.then_inc(src_ready, 1)

            def message(m):
                def stage(g):
                    dve.wait_ge(h_kept, g.n * H + m + 1)
                    dve.wait_ge(w_ps, g.n * H + m + 1)
                    wait(dve, msgl_sb, (g.n - 1) * H + m + 1)
                    dve.scalar_tensor_tensor(out=msg[:, m], in0=bank[5][:], scalar=bias_w[:, m:m + 1], in1=h_sb[:, m],
                                             op0=ALU.add, op1=ALU.mult).then_inc(msg_sb, 1)
                return stage

            def msg_low(m):
                def stage(g):
                    dve.wait_ge(msgh_sb, g.n * H + m + 1)
                    wait(dve, m_ps, g.n * 2)
                    low(msg_l[:, m], msg[:, m].rearrange("f (r e) -> f r e", r=R), msg_h[:, m], msgl_sb)
                return stage

            def m_low(q):
                def stage(g):
                    wait(dve, y_ps, (g.n - 1) * 2 + q + 1)
                    dve.wait_ge(mh_sb, g.n * R + 2 * q + 2)
                    for k in range(2):
                        r = 2 * q + k
                        dve.scalar_tensor_tensor(out=m_l[0:g.p, r], in0=bank[6][0:g.p, k * D:(k + 1) * D], scalar=col(wgt_t, r, g),
                                                 in1=m_h[0:g.p, r].bitcast(F32), op0=ALU.mult, op1=ALU.subtract).then_inc(ml_sb, 1)
                return stage

            def softplus(h):
                def stage(g):
                    dve.wait_ge(ln_sb, g.n * H + h + 1)
                    wait(dve, sspl_sb, (g.n - 1) * H + h + 1)
                    dve.scalar_tensor_tensor(out=ssp[:, h], in0=bank[2 + h][:], scalar=neg_bf1[:, h:h + 1], in1=lnz[:, h],
                                             op0=ALU.max, op1=ALU.add).then_inc(ssp_sb, 1)
                return stage

            def ssp_low(h):
                def stage(g):
                    dve.wait_ge(ssph_sb, g.n * H + h + 1)
                    wait(dve, w_ps, (g.n - 1) * H)
                    low(ssp_l[:, g.par, h], ssp[:, h].rearrange("m (r e) -> m r e", r=R), ssp_h[:, g.par, h], sspl_sb)
                return stage

            run(dve, (message(0), 2), (x_low(1), 1), (target, 3), (softplus(0), 1), (softplus(1), 1), (msg_low(0), 2),
                (message(1), 2), (m_low(1), 3), (msg_low(1), 2), (ssp_low(0), 1), (a_low, 0), (ssp_low(1), 1), (compare, 2),
                (m_low(0), 2), (x_low(0), 0))

            def cap_2(g):
                for h in range(H):
                    dve.wait_ge(mt_ps, g.n * H + h + 1)
                    wait(dve, exp2, (g.n - 1) * H + h + 1)
                    dve.tensor_scalar(capped[:, h], bank[2 * g.par + h][:], bo1[:, h:h + 1], EXP_CAP, ALU.add, ALU.min).then_inc(cap2, 1)

            def softplus_2(g):
                wait(dve, o_ps, (g.n - 1) * 2)
                for h in range(H):
                    dve.wait_ge(ln2, g.n * H + h + 1)
                    dve.scalar_tensor_tensor(out=ssp2[:, g.par, h].rearrange("m r n -> m (r n)"), in0=bank[2 * g.par + h][:],
                                             scalar=bo1_less[:, h:h + 1], in1=lnz[:, h], op0=ALU.add, op1=ALU.max).then_inc(ssp2_sb, 1)

            def residual(g):
                dve.wait_ge(x_got[g.par], g.nth * 16)
                wait(dve, norm_sb, g.n - 1)
                for r in range(R):
                    if r % 2 == 0:
                        dve.wait_ge(o_ps, g.n * 2 + r // 2 + 1)
                    last = dve.scalar_tensor_tensor(out=res[0:g.p, g.par, r], in0=x_in[0:g.p, g.par, r], scalar=2.0,
                                                    in1=bank[4 + 2 * g.par + r // 2][0:g.p, (r % 2) * D:(r % 2 + 1) * D],
                                                    op0=ALU.mult, op1=ALU.add, accum_out=total[0:g.p, g.par, r:r + 1])
                last.then_inc(res_sb, 1)
                dve.wait_ge(res_sb, g.n + 1)
                dve.tensor_scalar(neg_mean[0:g.p, g.par], total[0:g.p, g.par], -1.0 / D, None, ALU.mult).then_inc(mean_sb, 1)

            def variance(g):
                dve.wait_ge(square_sb, g.n + 1)
                dve.tensor_scalar(veps[0:g.p, g.par], square[0:g.p, g.par], 1.0 / D, EPS, ALU.mult, ALU.add).then_inc(veps_sb, 1)

            run(dve, (cap_2, 0), (variance, 3), (residual, 2), (softplus_2, 0))


_OUT = (50000, 256)


def kernel(**inputs):
    import numpy as np
    import concourse.bacc as bacc
    from concourse.bass_utils import run_bass_kernel_spmd

    nc = bacc.Bacc("TRN2", target_bir_lowering=False, num_devices=1)
    arrays, t = {}, {}
    for name, value in inputs.items():
        a = np.ascontiguousarray(value)
        arrays[f"in_{name}"] = a
        t[name] = nc.dram_tensor(f"in_{name}", a.shape, mybir.dt.from_np(a.dtype), kind="ExternalInput").ap()
    out = nc.dram_tensor("out_0", _OUT, F32, kind="ExternalOutput").ap()
    build(nc, t, out)
    return run_bass_kernel_spmd(nc, [arrays], core_ids=[0]).results[0]["out_0"]
```

```python
from contextlib import ExitStack

import concourse.bass as bass
from concourse import mybir

ALU = mybir.AluOpType
ACT = mybir.ActivationFunctionType
F32 = mybir.dt.float32
F32R = mybir.dt.float32r
I32 = mybir.dt.int32

P = 128
R = 4
RING = 8
EARLY = 22
LOG2 = 0.6931471805599453
EXP_CAP = 40.0
EPS = 1e-5


class Group:

    def __init__(self, number, parity, nth, rows):
        self.n, self.par, self.nth, self.rows = number, parity, nth, rows
        self.p = rows // R
        early = isinstance(number, int) and number < EARLY
        self.slot = number % RING if early else parity
        self.last = number - (RING if early else 2)


def wait(eng, sem, value):
    if isinstance(value, int) and value <= 0:
        return
    eng.wait_ge(sem, value)


def build(nc, t, out):
    N, D = t["x"].shape
    E = t["src"].shape[0]
    A = t["edge_attr_64"].shape[1]
    H = D // P
    ROWS = R * P
    assert D == 2 * P and 2 * A == P and E == N and E % R == 0
    G = -(-E // ROWS)
    TAIL = E - (G - 1) * ROWS

    def group(n):
        return Group(n, n % 2, n // 2 + 1, ROWS if n < G - 1 else TAIL)

    def run(eng, *stages, peel=0, start=0):
        lags = [lag for _, lag in stages]
        first = max(max(lags) + 2, peel, start)
        first += (G - 1 - first) % 2
        rounds = (G - 1 - first) // 2

        def straight(steps):
            for s in steps:
                for stage, lag in stages:
                    if 0 <= s - lag < G:
                        stage(group(s - lag))

        straight(range(start, first))
        with eng.Fori(0, rounds) as i:
            for u in range(2):
                for stage, lag in stages:
                    k = first + u - lag
                    stage(Group(i * 2 + k, k % 2, i + (k // 2 + 1), ROWS))
        straight(range(first + 2 * rounds, G + max(lags)))

    acc = nc.dram_tensor("acc", [N + 2 * P, D], F32, kind="Internal").ap()

    with ExitStack() as ctx:
        def sb(name, shape, dt=F32):
            return ctx.enter_context(nc.sbuf_tensor(name, shape, dt))

        def sem(name):
            return ctx.enter_context(nc.semaphore(name))

        bank = [ctx.enter_context(nc.psum_tensor(f"bank{i}", [P, 512], F32)) for i in range(8)]

        ident = sb("ident", [P, P])
        before = sb("before", [P, 3, P])
        ones = sb("ones", [2, P])
        ones_r = sb("ones_r", [2, P], F32R)
        w_in, wf2, wo1, wo2 = (sb(n, [P, H, D]) for n in ("w_in", "wf2", "wo1", "wo2"))
        w_in_h, w_in_l, wf2_h, wf2_l, wo1_h, wo1_l = (
            sb(n, [P, H, D], F32R) for n in ("w_in_h", "w_in_l", "wf2_h", "wf2_l", "wo1_h", "wo1_l"))
        wf1 = sb("wf1", [P, D])
        wf1_h = sb("wf1_h", [P, D], F32R)
        wf1_hl = sb("wf1_hl", [P, D], F32R)
        bf1, bf2, bo1 = (sb(n, [P, H]) for n in ("bf1", "bf2", "bo1"))
        neg_bf1 = sb("neg_bf1", [P, H])
        bo1_less = sb("bo1_less", [P, H])
        bf1_two = sb("bf1_two", [P, H, 2])
        bias_w = sb("bias_w", [P, H])
        bo2 = sb("bo2", [2, D])
        bo2_h, bo2_l = sb("bo2_h", [2, D], F32R), sb("bo2_l", [2, D], F32R)
        bo2_hl = sb("bo2_hl", [2, D], F32R)
        rows_i = sb("rows_i", [P, ROWS], I32)
        rows_f = sb("rows_f", [P, 2, ROWS])
        src_t, wgt_t = (sb(n, [P, R, G]) for n in ("src_t", "wgt_t"))
        spare_i = sb("spare_i", [P, 1], I32)
        spare_f = sb("spare_f", [P, 2])
        to_spare = sb("to_spare", [P, R, G])
        half = sb("half", [P, 1])
        neg_half = sb("neg_half", [P, R])
        CLEAR = 2
        zeros = sb("zeros", [P, 4 * D])

        attr = sb("attr", [P, 2, R, 2, A])
        srcb = sb("srcb", [P, 2, ROWS], I32)
        xg = [[sb(f"xg{u}{r}", [P, D]) for r in range(R)] for u in range(2)]
        dst_ix = [sb(f"dst_ix{u}", [P, R], I32) for u in range(2)]
        src_ix = [[sb(f"src_ix{k}{r}", [P, 1], I32) for r in range(R)] for k in range(RING)]
        x_h, x_l = (sb(n, [P, 2, H, R, P], F32R) for n in ("x_h", "x_l"))
        a_h, a_l = (sb(n, [P, R, P], F32R) for n in ("a_h", "a_l"))
        absz, expz, lnz, ssp = (sb(n, [P, H, 512]) for n in ("absz", "expz", "lnz", "ssp"))
        ssp_h, ssp_l = (sb(n, [P, 2, H, R, P], F32R) for n in ("ssp_h", "ssp_l"))
        same = sb("same", [P, 2, 2, 3, P], F32R)
        junk = sb("junk", [P, 2, 3, P])
        earlier = sb("earlier", [P, 2, R])
        move = sb("move", [P, R])
        h_sb, msg = (sb(n, [P, H, 512]) for n in ("h_sb", "msg"))
        msg_h, msg_l = (sb(n, [P, H, R, P], F32R) for n in ("msg_h", "msg_l"))
        m_h, m_l = (sb(n, [P, R, D], F32R) for n in ("m_h", "m_l"))
        y = sb("y", [P, 2, R, D])

        m_in, x_in, res = (sb(n, [P, 2, R, D]) for n in ("m_in", "x_in", "res"))
        capped, normed, squares = absz, y, msg
        sums = [b[:, u] for b in (y, m_in, x_in, res) for u in range(2)]
        assert len(sums) == RING
        ssp2 = sb("ssp2", [P, 2, H, R, P])
        total, neg_mean, square, veps, rstd = (sb(n, [P, 2, R]) for n in ("total", "neg_mean", "square", "veps", "rstd"))

        dve_own = sem("dve_own")
        const_in = sem("const_in")
        rows_in = sem("rows_in")
        rows_zero = sem("rows_zero")
        zeros_made = sem("zeros_made")
        rows_cast = sem("rows_cast")
        made = sem("made")
        cleared = sem("cleared")
        tab_ps = sem("tab_ps")
        tab_sb = sem("tab_sb")
        two_made = sem("two_made")
        bias_ps = sem("bias_ps")
        const_made = sem("const_made")
        attr_in = [sem(f"attr_in{u}") for u in range(2)]
        srcb_in = [sem(f"srcb_in{u}") for u in range(2)]
        xg_in = [[sem(f"xg_in{u}{r}") for r in range(R)] for u in range(2)]
        added = sem("added")
        dst_in = [sem(f"dst_in{u}") for u in range(2)]
        src_ready = sem("src_ready")
        same_ready = sem("same_ready")
        earlier_ready, move_ready = sem("earlier_ready"), sem("move_ready")
        xt_ps = sem("xt_ps")
        xh_sb, xl_sb = sem("xh_sb"), sem("xl_sb")
        at_ps = sem("at_ps")
        ah_sb, al_sb = sem("ah_sb"), sem("al_sb")
        z_ps = sem("z_ps")
        abs_sb, exp_sb, ln_sb, ssp_sb, ssph_sb, sspl_sb = (
            sem(n) for n in ("abs_sb", "exp_sb", "ln_sb", "ssp_sb", "ssph_sb", "sspl_sb"))
        h_ps, w_ps = sem("h_ps"), sem("w_ps")
        h_kept = sem("h_kept")
        msg_sb = sem("msg_sb")
        msgh_sb, msgl_sb = sem("msgh_sb"), sem("msgl_sb")
        m_ps = sem("m_ps")
        mh_sb, ml_sb = sem("mh_sb"), sem("ml_sb")
        y_ps, y_sb = sem("y_ps"), sem("y_sb")
        pool_step, sp_step = sem("pool_step"), sem("sp_step")
        m_got = [sem(f"m_got{u}") for u in range(2)]
        x_got = [sem(f"x_got{u}") for u in range(2)]
        mt_ps = sem("mt_ps")
        cap2, exp2, ln2, ssp2_sb = (sem(n) for n in ("cap2", "exp2", "ln2", "ssp2_sb"))
        o_ps = sem("o_ps")
        res_sb, mean_sb = sem("res_sb"), sem("mean_sb")
        square_sb = sem("square_sb")
        veps_sb = sem("veps_sb")
        rstd_sb, norm_sb = sem("rstd_sb"), sem("norm_sb")
        stored = [sem(f"stored{u}") for u in range(2)]

        SCATTERS_FROM = 9
        CAUGHT_UP = EARLY + 7
        assert (CAUGHT_UP - SCATTERS_FROM) * 5 // 2 >= (CAUGHT_UP - 6) * 2 + 1

        block = ctx.enter_context(nc.Block())

        CONSTS = 13
        CLEARS = N // P // CLEAR
        CLEARS_A_STEP = 20
        assert N // P % CLEAR == 0

        def rows_of(ap, g):
            return ap[bass.ds(g.n * ROWS, g.rows)]

        def col(table, r, g):
            return table[0:g.p, r, bass.ds(g.n, 1)]

        @block.sync
        def _(sp):
            sp.wait_ge(rows_zero, 1)
            flat = t["edge_weight1"].rearrange("e a -> (e a)")
            for dest, ap in ((rows_i, t["src"]), (rows_f[:, 1], flat)):
                sp.dma_start(dest[0:G - 1, :], ap[0:(G - 1) * ROWS].rearrange("(g e) -> g e", e=ROWS)).then_inc(rows_in, 16)
                sp.dma_start(dest[G - 1:G, 0:TAIL], ap[(G - 1) * ROWS:E].rearrange("(g e) -> g e", e=TAIL)).then_inc(rows_in, 16)
            for k in range(2):
                sp.dma_start(wf1[k * A:(k + 1) * A, :], t["L0_gnn_Wf1"]).then_inc(const_in, 16)
            for w, name in ((w_in, "L0_gnn_W_in2f"), (wf2, "L0_gnn_Wf2"), (wo1, "L0_gnn_Wo1"), (wo2, "L0_gnn_Wo2")):
                sp.dma_start(w[:], t[name].rearrange("(h p) n -> p h n", p=P)).then_inc(const_in, 16)
            for b, name in ((bf1, "L0_gnn_bf1"), (bf2, "L0_gnn_bf2"), (bo1, "L0_gnn_bo1")):
                for h in range(H):
                    sp.dma_start(b[:, h:h + 1], t[name][h * P:(h + 1) * P].rearrange("(p a) -> p a", a=1)).then_inc(const_in, 16)
            sp.dma_start(bo2[:], t["L0_gnn_bo2"].partition_broadcast(2)).then_inc(const_in, 16)

            def load_dst(g):
                wait(sp, xt_ps, (g.n - 1) * 2)
                sp.sem_inc(sp_step, 1)
                sp.dma_start(dst_ix[g.par][0:g.p], rows_of(t["dst"], g).rearrange("(p r) -> p r", r=R)).then_inc(dst_in[g.par], 16)

            def load_attr(g):
                wait(sp, at_ps, g.n - 1)
                sp.sem_inc(sp_step, 1)
                for k in range(2):
                    sp.dma_start(attr[0:g.p, g.par, :, k, :], rows_of(t["edge_attr_64"], g).rearrange("(p r) a -> p r a", r=R)).then_inc(attr_in[g.par], 16)

            def load_src(g):
                wait(sp, same_ready, (g.n - 1) * R)
                sp.sem_inc(sp_step, 1)
                sp.dma_start(srcb[:, g.par, 0:g.rows], rows_of(t["src"], g).partition_broadcast(P)).then_inc(srcb_in[g.par], 16)

            def clear(g):
                if isinstance(g.n, int) and g.n * CLEARS_A_STEP <= CLEARS:
                    for c in range(g.n * CLEARS_A_STEP, min((g.n + 1) * CLEARS_A_STEP, CLEARS)):
                        sp.dma_start(acc[c * CLEAR * P:(c + 1) * CLEAR * P, :].rearrange("(p k) d -> p (k d)", k=CLEAR), zeros[:, 0:CLEAR * D]).then_inc(cleared, 16)
                    if (g.n + 1) * CLEARS_A_STEP > CLEARS:
                        rest = N + 2 * P - CLEARS * CLEAR * P
                        sp.dma_start(acc[CLEARS * CLEAR * P:N + 2 * P, :].rearrange("(p k) d -> p (k d)", k=4), zeros[0:rest // 4, 0:4 * D]).then_inc(cleared, 16)

            sp.wait_ge(zeros_made, 1)
            run(sp, (load_dst, 0), (load_attr, 0), (load_src, 2), (clear, 0), peel=CLEARS // CLEARS_A_STEP + 1)

            sp.wait_ge(added, 16 * R * G)

            def fetch_m(g):
                wait(sp, mt_ps, (g.n - 1) * H)
                sp.sem_inc(sp_step, 1)
                sp.dma_start(m_in[0:g.p, g.par].rearrange("p r d -> p (r d)"), rows_of(acc, g).rearrange("(p r) d -> p (r d)", r=R)).then_inc(m_got[g.par], 16)

            def fetch_x(g):
                wait(sp, res_sb, g.n - 1)
                sp.sem_inc(sp_step, 1)
                sp.dma_start(x_in[0:g.p, g.par].rearrange("p r d -> p (r d)"), rows_of(t["x"], g).rearrange("(p r) d -> p (r d)", r=R)).then_inc(x_got[g.par], 16)

            def store(g):
                wait(sp, norm_sb, g.n + 1)
                sp.sem_inc(sp_step, 1)
                sp.dma_start(rows_of(out, g).rearrange("(p r) d -> p (r d)", r=R), normed[0:g.p, g.par].rearrange("p r d -> p (r d)")).then_inc(stored[g.par], 16)

            run(sp, (fetch_m, 0), (fetch_x, 1), (store, 5))
            for u in range(2):
                sp.wait_ge(stored[u], 16 * len(range(u, G, 2)))

        @block.gpsimd
        def _(pool):
            pool.memset(ident[:], 0.0).then_inc(pool_step, 1)
            pool.memset(before[:], 1.0).then_inc(pool_step, 1)
            pool.memset(neg_half[:], -0.5).then_inc(made, 1)
            pool.memset(half[:], 0.5).then_inc(made, 1)
            pool.memset(ones[:], 1.0).then_inc(made, 1)
            pool.iota(spare_i[:], [[0, 1]], base=N, channel_multiplier=1).then_inc(made, 1)
            pool.wait_ge(pool_step, 2)
            pool.affine_select(out=ident[:], in_=ident[:], compare_op=ALU.not_equal, fill=1.0, base=0,
                               pattern=[[-1, P]], channel_multiplier=1).then_inc(made, 1)
            for k in (0, 2):
                pool.affine_select(out=before[:, k], in_=before[:, k], compare_op=ALU.is_gt, fill=0.0, base=0,
                                   pattern=[[-1, P]], channel_multiplier=1).then_inc(made, 1)
            pool.memset(zeros[:], 0.0).then_inc(zeros_made, 1)

            def gather(r):
                def stage(g):
                    pool.wait_ge(dst_in[g.par], g.nth * 16)
                    wait(pool, xt_ps, (g.n - 1) * 2)
                    pool.sem_inc(pool_step, 1)
                    pool.indirect_dma_start(xg[g.par][r][0:g.p, :], None, t["x"],
                                            bass.IndirectOffsetOnAxis(ap=dst_ix[g.par][0:g.p, r:r + 1], axis=0)).then_inc(xg_in[g.par][r], 16)
                return stage

            def scatter(r):
                def stage(g):
                    if isinstance(g.n, int) and g.n == 0 and r == 0:
                        pool.wait_ge(cleared, 16 * (CLEARS + 1))
                    wait(pool, src_ready, g.n + 1)
                    wait(pool, y_sb, g.n * 2 + r // 2 + 1)
                    if r % 2 == 0:
                        wait(pool, added, (g.n * R + r) * 16)
                    pool.sem_inc(pool_step, 1)
                    pool.indirect_dma_start(acc, bass.IndirectOffsetOnAxis(ap=src_ix[g.slot][r][0:g.p, :], axis=0),
                                            sums[g.slot][0:g.p, r], None, compute_op=ALU.add).then_inc(added, 16)
                return stage

            pairs = 0
            for s in range(CAUGHT_UP):
                pairs_now = max(0, min((s - 5) * 2 + 1, (s + 1 - SCATTERS_FROM) * 5 // 2))
                todo = pairs_now - pairs
                for r in range(R):
                    for pair in range(pairs + r * todo // R, pairs + (r + 1) * todo // R):
                        for k in range(2):
                            scatter(pair % 2 * 2 + k)(group(pair // 2))
                    gather(r)(group(s))
                pairs = pairs_now
            run(pool, (scatter(2), 6), (scatter(3), 6), (gather(0), 0), (gather(1), 0), (scatter(0), 5), (scatter(1), 5),
                (gather(2), 0), (gather(3), 0), start=CAUGHT_UP)

            def norm(g):
                pool.wait_ge(veps_sb, g.n + 1)
                pool.tensor_tensor(rstd[0:g.p, g.par], veps[0:g.p, g.par], neg_half[0:g.p], ALU.pow).then_inc(rstd_sb, 1)
                pool.wait_ge(rstd_sb, g.n + 1)
                if not isinstance(g.n, int) or g.n >= 2:
                    pool.wait_ge(stored[g.par], (g.nth - 1) * 16)
                pool.sem_inc(pool_step, 1)
                for r in range(R):
                    last = pool.tensor_scalar(normed[0:g.p, g.par, r], res[0:g.p, g.par, r], neg_mean[0:g.p, g.par, r:r + 1],
                                              rstd[0:g.p, g.par, r:r + 1], ALU.add, ALU.mult)
                last.then_inc(norm_sb, 1)

            run(pool, (norm, 0))

        @block.tensor
        def _(pe):
            pe.wait_ge(made, 7)
            pe.wait_ge(rows_cast, 1)
            for k in range(2):
                if k == 1:
                    pe.wait_ge(rows_in, 16 * 4)
                for r in range(R):
                    last = pe.transpose(bank[k][:, r * G:(r + 1) * G], rows_f[0:G, k, r::R], ident[0:G, 0:G])
                last.then_inc(tab_ps, 1)
            pe.wait_ge(two_made, 1)
            for m in range(H):
                for k in range(H):
                    last = pe.matmul(bank[3][:, 2 * m:2 * m + 2], wf2[:, k, m * P:(m + 1) * P], bf1_two[:, k], start=k == 0, stop=k == H - 1)
            last.then_inc(bias_ps, 1)
            pe.wait_ge(tab_sb, 2)

            def three(o, stat_h, stat_l, mov_h, mov_l):
                terms = [ab for sh, sl, mh, ml in zip(stat_h, stat_l, mov_h, mov_l) for ab in ((sh, mh), (sh, ml), (sl, mh))]
                for n, (a, b) in enumerate(terms):
                    last = pe.matmul(o, a, b, start=n == 0, stop=n == len(terms) - 1)
                return last

            def turn_x(q):
                def stage(g):
                    for k in range(2):
                        pe.wait_ge(xg_in[g.par][2 * q + k], g.nth * 16)
                    wait(pe, xl_sb, (g.n - 1) * 2 + q + 1)
                    for h in range(H):
                        for k in range(2):
                            c = (h * 2 + k) * P
                            last = pe.transpose(bank[q][:, c:c + g.p], xg[g.par][2 * q + k][0:g.p, h * P:(h + 1) * P], ident[0:g.p, 0:g.p])
                    last.then_inc(xt_ps, 1)
                return stage

            def turn_a(g):
                pe.wait_ge(attr_in[g.par], g.nth * 32)
                wait(pe, ssp_sb, g.n * H)
                for r in range(R):
                    last = pe.transpose(bank[2][:, r * P:r * P + g.p],
                                        attr[0:g.p, g.par, r].rearrange("e k a -> e (k a)"), ident[0:g.p, 0:g.p])
                last.then_inc(at_ps, 1)

            def filter1(g):
                pe.wait_ge(al_sb, g.n + 1)
                wait(pe, ssp_sb, g.n * H)
                for h in range(H):
                    o = bank[2 + h][:].rearrange("m (r e) -> m r e", r=R)[:, :, 0:g.p]
                    pe.matmul(o, wf1_hl[:, h * P:(h + 1) * P], a_h[:, :, 0:g.p], start=True, stop=False)
                    last = pe.matmul(o, wf1_hl[:, h * P:(h + 1) * P], a_l[:, :, 0:g.p], start=False, stop=True)
                last.then_inc(z_ps, 1)

            def transposed(m, psum, w_h, w_l, in_h, in_l):
                cols = slice(m * P, (m + 1) * P)
                return three(psum, [w_h[:, k, cols] for k in range(H)], [w_l[:, k, cols] for k in range(H)], in_h, in_l)

            def h_of(m):
                def stage(g):
                    if m == 0:
                        pe.wait_ge(xl_sb, g.n * 2 + 2)
                    wait(pe, h_kept, g.n * H + m)
                    transposed(m, bank[4][:].rearrange("f (r e) -> f r e", r=R)[:, :, 0:g.p], w_in_h, w_in_l,
                               [x_h[:, g.par, k, :, 0:g.p] for k in range(H)], [x_l[:, g.par, k, :, 0:g.p] for k in range(H)]).then_inc(h_ps, 1)
                return stage

            def w_of(m):
                def stage(g):
                    if m == 0:
                        pe.wait_ge(sspl_sb, g.n * H + H)
                    wait(pe, msg_sb, g.n * H + m)
                    transposed(m, bank[5][:].rearrange("f (r e) -> f r e", r=R)[:, :, 0:g.p], wf2_h, wf2_l,
                               [ssp_h[:, g.par, k, :, 0:g.p] for k in range(H)], [ssp_l[:, g.par, k, :, 0:g.p] for k in range(H)]).then_inc(w_ps, 1)
                return stage

            def out1(q):
                def stage(g):
                    if q == 0:
                        pe.wait_ge(msgl_sb, g.n * H + H)
                    wait(pe, ml_sb, g.n * R + 2 * q)
                    for k in range(2):
                        last = three(bank[6][0:g.p, k * D:(k + 1) * D],
                                     [msg_h[:, h, 2 * q + k, 0:g.p] for h in range(H)], [msg_l[:, h, 2 * q + k, 0:g.p] for h in range(H)],
                                     [wo1_h[:, h] for h in range(H)], [wo1_l[:, h] for h in range(H)])
                    last.then_inc(m_ps, 1)
                return stage

            def summed(q):
                def stage(g):
                    pe.wait_ge(ml_sb, g.n * R + 2 * q + 2)
                    if q == 0:
                        pe.wait_ge(same_ready, g.n * R + R)
                    wait(pe, y_sb, g.n * 2 + q)
                    for k in range(2):
                        o = bank[7][0:g.p, k * D:(k + 1) * D]
                        terms = [(b, m, r) for b, r in (((0, 2 * q), (1, 2 * q + 1)) if k == 0 else ((2, 2 * q + 1),)) for m in (m_h, m_l)]
                        for n, (b, m, r) in enumerate(terms):
                            last = pe.matmul(o, same[0:g.p, g.par, q, b, 0:g.p], m[0:g.p, r], start=n == 0, stop=n == len(terms) - 1)
                    last.then_inc(y_ps, 1)
                return stage

            pe.wait_ge(const_made, 1)
            run(pe, (w_of(1), 2), (turn_a, 0), (summed(0), 3), (h_of(0), 1), (summed(1), 3), (filter1, 0), (turn_x(0), 0),
                (out1(0), 2), (turn_x(1), 0), (w_of(0), 1), (h_of(1), 1), (out1(1), 2))

            def turn2(g):
                pe.wait_ge(m_got[g.par], g.nth * 16)
                wait(pe, ssp2_sb, (g.n - 1) * H)
                for h in range(H):
                    for r in range(R):
                        last = pe.transpose(bank[2 * g.par + h][:, r * P:r * P + g.p], m_in[0:g.p, g.par, r, h * P:(h + 1) * P], ident[0:g.p, 0:g.p])
                    last.then_inc(mt_ps, 1)

            def out2(g):
                pe.wait_ge(ssp2_sb, g.n * H + H)
                wait(pe, res_sb, g.n - 1)
                for q in range(2):
                    for k in range(2):
                        o = bank[4 + 2 * g.par + q][0:g.p, k * D:(k + 1) * D]
                        for h in range(H):
                            pe.matmul(o, ssp2[:, g.par, h, 2 * q + k, 0:g.p], wo2[:, h, :], start=h == 0, stop=False)
                        last = pe.matmul(o, ones_r[:, 0:g.p], bo2_hl[:], start=False, stop=True)
                    last.then_inc(o_ps, 1)

            run(pe, (turn2, 0), (out2, 1))

        @block.scalar
        def _(act):
            act.preload_act_table_set("natural_log_exp_and_others")

            def high(out_, in_, done):
                act.activation(out_, in_, ACT.Copy).then_inc(done, 1)

            def x_high(q):
                def stage(g):
                    act.wait_ge(xt_ps, g.n * 2 + q + 1)
                    wait(act, h_ps, (g.n - 1) * H)
                    high(x_h[:, g.par, :, 2 * q:2 * q + 2, 0:g.p], bank[q][:].rearrange("f (h k e) -> f h k e", h=H, k=2)[:, :, :, 0:g.p], xh_sb)
                return stage

            def a_high(g):
                act.wait_ge(at_ps, g.n + 1)
                wait(act, z_ps, g.n)
                high(a_h[:, :, 0:g.p], bank[2][:].rearrange("f (r e) -> f r e", r=R)[:, :, 0:g.p], ah_sb)

            def absolute(h):
                def stage(g):
                    act.wait_ge(z_ps, g.n + 1)
                    act.activation(absz[:, h], bank[2 + h][:], ACT.Abs, bias=bf1[:, h:h + 1]).then_inc(abs_sb, 1)
                return stage

            def expo(h):
                def stage(g):
                    act.wait_ge(abs_sb, g.n * H + h + 1)
                    act.activation(expz[:, h], absz[:, h], ACT.Exp, scale=-1.0).then_inc(exp_sb, 1)
                return stage

            def loga(h):
                def stage(g):
                    act.wait_ge(exp_sb, g.n * H + h + 1)
                    wait(act, ssp_sb, (g.n - 1) * H + h + 1)
                    act.activation(lnz[:, h], expz[:, h], ACT.Ln, bias=half[:], scale=0.5).then_inc(ln_sb, 1)
                return stage

            def ssp_high(h):
                def stage(g):
                    act.wait_ge(ssp_sb, g.n * H + h + 1)
                    wait(act, w_ps, (g.n - 1) * H)
                    high(ssp_h[:, g.par, h], ssp[:, h].rearrange("m (r e) -> m r e", r=R), ssph_sb)
                return stage

            def keep_h(m):
                def stage(g):
                    act.wait_ge(h_ps, g.n * H + m + 1)
                    wait(act, msg_sb, (g.n - 1) * H + m + 1)
                    act.activation(h_sb[:, m], bank[4][:], ACT.Copy).then_inc(h_kept, 1)
                return stage

            def msg_high(m):
                def stage(g):
                    act.wait_ge(msg_sb, g.n * H + m + 1)
                    wait(act, m_ps, g.n * 2)
                    high(msg_h[:, m], msg[:, m].rearrange("f (r e) -> f r e", r=R), msgh_sb)
                return stage

            def m_high(q):
                def stage(g):
                    act.wait_ge(m_ps, g.n * 2 + q + 1)
                    wait(act, y_ps, (g.n - 1) * 2 + q + 1)
                    for k in range(2):
                        r = 2 * q + k
                        act.activation(m_h[0:g.p, r], bank[6][0:g.p, k * D:(k + 1) * D], ACT.Copy, scale=col(wgt_t, r, g)).then_inc(mh_sb, 1)
                return stage

            def keep_y(q):
                def stage(g):
                    act.wait_ge(y_ps, g.n * 2 + q + 1)
                    wait(act, added, (g.last * R + 2 * q + 2) * 16)
                    act.activation(sums[g.slot][0:g.p, 2 * q:2 * q + 2].rearrange("e k d -> e (k d)"), bank[7][0:g.p], ACT.Copy).then_inc(y_sb, 1)
                return stage

            act.wait_ge(const_made, 1)
            run(act, (keep_y(0), 4), (msg_high(1), 3), (ssp_high(0), 2), (ssp_high(1), 2), (keep_h(0), 2), (absolute(0), 1),
                (absolute(1), 1), (expo(0), 1), (m_high(0), 3), (keep_y(1), 4), (expo(1), 1), (x_high(0), 1), (loga(0), 1),
                (loga(1), 1), (x_high(1), 1), (keep_h(1), 2), (m_high(1), 3), (a_high, 0), (msg_high(0), 2), peel=EARLY + 4)

            def softplus2(g):
                for h in range(H):
                    act.wait_ge(cap2, g.n * H + h + 1)
                    act.activation(expz[:, h], capped[:, h], ACT.Exp).then_inc(exp2, 1)
                for h in range(H):
                    act.wait_ge(exp2, g.n * H + h + 1)
                    wait(act, ssp2_sb, (g.n - 1) * H + h + 1)
                    act.activation(lnz[:, h], expz[:, h], ACT.Ln, bias=half[:], scale=0.5).then_inc(ln2, 1)

            def deviation(g):
                act.wait_ge(mean_sb, g.n + 1)
                wait(act, veps_sb, g.n - 1)
                for r in range(R):
                    last = act.activation(squares[0:g.p, r // 2, r % 2 * D:(r % 2 + 1) * D], res[0:g.p, g.par, r], ACT.Square,
                                          bias=neg_mean[0:g.p, g.par, r:r + 1], accum_out=square[0:g.p, g.par, r:r + 1])
                last.then_inc(square_sb, 1)

            run(act, (softplus2, 0), (deviation, 2))

        @block.vector
        def _(dve):
            dve.memset(rows_i[:], 0).then_inc(dve_own, 1)
            dve.memset(rows_f[:, 1], 0.0).then_inc(dve_own, 1)
            dve.wait_ge(dve_own, 2)
            dve.sem_inc(rows_zero, 1)
            dve.wait_ge(rows_in, 16 * 4)
            dve.tensor_copy(rows_f[:, 0], rows_i[:]).then_inc(rows_cast, 1)
            dve.wait_ge(made, 7)
            dve.tensor_copy(spare_f[:, 0:1], spare_i[:]).then_inc(dve_own, 1)
            dve.tensor_scalar(spare_f[:, 1:2], spare_i[:], float(P), None, ALU.add).then_inc(dve_own, 1)
            for k, table in enumerate((src_t, wgt_t)):
                dve.wait_ge(tab_ps, k + 1)
                dve.tensor_copy(table[:].rearrange("p r g -> p (r g)"), bank[k][:, 0:R * G]).then_inc(dve_own, 1)
            dve.wait_ge(dve_own, 6)
            for k in range(2):
                dve.tensor_scalar(to_spare[:, k::2], src_t[:, k::2], -1.0, spare_f[:, k:k + 1], ALU.mult, ALU.add).then_inc(tab_sb, 1)

            def low(out_, whole, high, done, count=1):
                dve.tensor_tensor(out_, whole, high.bitcast(F32), ALU.subtract).then_inc(done, count)

            dve.wait_ge(const_in, 16 * CONSTS)
            for k in range(2):
                dve.tensor_copy(bf1_two[:, :, k], bf1[:]).then_inc(dve_own, 1)
            dve.wait_ge(dve_own, 8)
            dve.sem_inc(two_made, 1)
            for w, wh in ((w_in, w_in_h), (wf2, wf2_h), (wo1, wo1_h), (wf1, wf1_h), (bo2, bo2_h)):
                dve.tensor_copy(wh[:], w[:]).then_inc(dve_own, 1)
            dve.tensor_copy(wf1_hl[0:A], wf1[0:A]).then_inc(dve_own, 1)
            dve.tensor_copy(ones_r[:], ones[:]).then_inc(dve_own, 1)
            dve.tensor_scalar(neg_bf1[:], bf1[:], -1.0, None, ALU.mult).then_inc(dve_own, 1)
            dve.tensor_scalar(bo1_less[:], bo1[:], LOG2, None, ALU.subtract).then_inc(dve_own, 1)
            dve.wait_ge(dve_own, 17)
            for w, wh, wl in ((w_in, w_in_h, w_in_l), (wf2, wf2_h, wf2_l), (wo1, wo1_h, wo1_l), (bo2, bo2_h, bo2_l)):
                low(wl[:], w[:], wh[:], dve_own)
            low(wf1_hl[A:P], wf1[A:P], wf1_h[A:P], dve_own)
            dve.wait_ge(bias_ps, 1)
            dve.tensor_tensor(bias_w[:], bf2[:], bank[3][:, 0:2 * H:2], ALU.add).then_inc(dve_own, 1)
            dve.wait_ge(dve_own, 23)
            dve.tensor_scalar(bo2[:], bo2_l[:].bitcast(F32), ident[0:2, 1:2], None, ALU.mult).then_inc(dve_own, 1)
            dve.wait_ge(dve_own, 24)
            dve.scalar_tensor_tensor(out=bo2_hl[:], in0=bo2_h[:].bitcast(F32), scalar=ident[0:2, 0:1], in1=bo2[:],
                                     op0=ALU.mult, op1=ALU.add).then_inc(const_made, 1)

            def x_low(q):
                def stage(g):
                    dve.wait_ge(xh_sb, g.n * 2 + q + 1)
                    wait(dve, h_ps, (g.n - 1) * H)
                    low(x_l[:, g.par, :, 2 * q:2 * q + 2, 0:g.p], bank[q][:].rearrange("f (h k e) -> f h k e", h=H, k=2)[:, :, :, 0:g.p],
                        x_h[:, g.par, :, 2 * q:2 * q + 2, 0:g.p], xl_sb)
                return stage

            def a_low(g):
                dve.wait_ge(ah_sb, g.n + 1)
                wait(dve, z_ps, g.n)
                low(a_l[:, :, 0:g.p], bank[2][:].rearrange("f (r e) -> f r e", r=R)[:, :, 0:g.p], a_h[:, :, 0:g.p], al_sb)

            def compare(g):
                dve.wait_ge(srcb_in[g.par], g.nth * 16)
                wait(dve, y_ps, (g.n - 1) * 2)
                sources = srcb[0:g.p, g.par, 0:R * g.p].rearrange("x (e r) -> x r e", r=R)
                blocks = ((0, slice(0, 1)), (1, slice(1, 3)))
                for q in range(2):
                    for k, b in blocks:
                        dve.tensor_scalar(same[0:g.p, g.par, q, b, 0:g.p], sources[:, 2 * q:2 * q + 1 + k], col(src_t, 2 * q + k, g), None,
                                          ALU.is_equal).then_inc(same_ready, 1)
                dve.wait_ge(same_ready, g.n * R + R)
                for q in range(2):
                    for k, b in blocks:
                        dve.tensor_tensor_reduce(out=junk[0:g.p, q, b, 0:g.p], in0=same[0:g.p, g.par, q, b, 0:g.p].bitcast(F32),
                                                 in1=before[0:g.p, b, 0:g.p], scale=1.0, scalar=0.0, op0=ALU.mult, op1=ALU.add,
                                                 accum_out=earlier[0:g.p, g.par, 2 * q + k:2 * q + k + 1]).then_inc(earlier_ready, 1)

            def target(g):
                dve.wait_ge(earlier_ready, g.n * R + R)
                dve.scalar_tensor_tensor(out=move[0:g.p], in0=earlier[0:g.p, g.par], scalar=0.0,
                                         in1=to_spare[0:g.p, :, bass.ds(g.n, 1)].squeeze(2), op0=ALU.is_gt, op1=ALU.mult).then_inc(move_ready, 1)
                dve.wait_ge(move_ready, g.n + 1)
                wait(dve, added, (g.last + 1) * R * 16)
                for r in range(R):
                    last = dve.tensor_tensor(src_ix[g.slot][r][0:g.p], move[0:g.p, r:r + 1], col(src_t, r, g), ALU.add)
                last.then_inc(src_ready, 1)

            def message(m):
                def stage(g):
                    dve.wait_ge(h_kept, g.n * H + m + 1)
                    dve.wait_ge(w_ps, g.n * H + m + 1)
                    wait(dve, msgl_sb, (g.n - 1) * H + m + 1)
                    dve.scalar_tensor_tensor(out=msg[:, m], in0=bank[5][:], scalar=bias_w[:, m:m + 1], in1=h_sb[:, m],
                                             op0=ALU.add, op1=ALU.mult).then_inc(msg_sb, 1)
                return stage

            def msg_low(m):
                def stage(g):
                    dve.wait_ge(msgh_sb, g.n * H + m + 1)
                    wait(dve, m_ps, g.n * 2)
                    low(msg_l[:, m], msg[:, m].rearrange("f (r e) -> f r e", r=R), msg_h[:, m], msgl_sb)
                return stage

            def m_low(q):
                def stage(g):
                    wait(dve, y_ps, (g.n - 1) * 2 + q + 1)
                    dve.wait_ge(mh_sb, g.n * R + 2 * q + 2)
                    for k in range(2):
                        r = 2 * q + k
                        dve.scalar_tensor_tensor(out=m_l[0:g.p, r], in0=bank[6][0:g.p, k * D:(k + 1) * D], scalar=col(wgt_t, r, g),
                                                 in1=m_h[0:g.p, r].bitcast(F32), op0=ALU.mult, op1=ALU.subtract).then_inc(ml_sb, 1)
                return stage

            def softplus(h):
                def stage(g):
                    dve.wait_ge(ln_sb, g.n * H + h + 1)
                    wait(dve, sspl_sb, (g.n - 1) * H + h + 1)
                    dve.scalar_tensor_tensor(out=ssp[:, h], in0=bank[2 + h][:], scalar=neg_bf1[:, h:h + 1], in1=lnz[:, h],
                                             op0=ALU.max, op1=ALU.add).then_inc(ssp_sb, 1)
                return stage

            def ssp_low(h):
                def stage(g):
                    dve.wait_ge(ssph_sb, g.n * H + h + 1)
                    wait(dve, w_ps, (g.n - 1) * H)
                    low(ssp_l[:, g.par, h], ssp[:, h].rearrange("m (r e) -> m r e", r=R), ssp_h[:, g.par, h], sspl_sb)
                return stage

            run(dve, (m_low(0), 3), (message(0), 2), (x_low(0), 1), (softplus(0), 1), (softplus(1), 1), (x_low(1), 1),
                (m_low(1), 3), (message(1), 2), (a_low, 0), (msg_low(0), 2), (target, 3), (msg_low(1), 2), (ssp_low(0), 1),
                (ssp_low(1), 1), (compare, 2), peel=EARLY + 3)

            def cap_2(g):
                for h in range(H):
                    dve.wait_ge(mt_ps, g.n * H + h + 1)
                    wait(dve, exp2, (g.n - 1) * H + h + 1)
                    dve.tensor_scalar(capped[:, h], bank[2 * g.par + h][:], bo1[:, h:h + 1], EXP_CAP, ALU.add, ALU.min).then_inc(cap2, 1)

            def softplus_2(g):
                wait(dve, o_ps, (g.n - 1) * 2)
                for h in range(H):
                    dve.wait_ge(ln2, g.n * H + h + 1)
                    dve.scalar_tensor_tensor(out=ssp2[:, g.par, h].rearrange("m r n -> m (r n)"), in0=bank[2 * g.par + h][:],
                                             scalar=bo1_less[:, h:h + 1], in1=lnz[:, h], op0=ALU.add, op1=ALU.max).then_inc(ssp2_sb, 1)

            def residual(g):
                dve.wait_ge(x_got[g.par], g.nth * 16)
                wait(dve, norm_sb, g.n - 1)
                for r in range(R):
                    if r % 2 == 0:
                        dve.wait_ge(o_ps, g.n * 2 + r // 2 + 1)
                    last = dve.scalar_tensor_tensor(out=res[0:g.p, g.par, r], in0=x_in[0:g.p, g.par, r], scalar=2.0,
                                                    in1=bank[4 + 2 * g.par + r // 2][0:g.p, (r % 2) * D:(r % 2 + 1) * D],
                                                    op0=ALU.mult, op1=ALU.add, accum_out=total[0:g.p, g.par, r:r + 1])
                last.then_inc(res_sb, 1)
                dve.wait_ge(res_sb, g.n + 1)
                dve.tensor_scalar(neg_mean[0:g.p, g.par], total[0:g.p, g.par], -1.0 / D, None, ALU.mult).then_inc(mean_sb, 1)

            def variance(g):
                dve.wait_ge(square_sb, g.n + 1)
                dve.tensor_scalar(veps[0:g.p, g.par], square[0:g.p, g.par], 1.0 / D, EPS, ALU.mult, ALU.add).then_inc(veps_sb, 1)

            run(dve, (cap_2, 0), (variance, 3), (residual, 2), (softplus_2, 0))


_OUT = (50000, 256)


def kernel(**inputs):
    import numpy as np
    import concourse.bacc as bacc
    from concourse.bass_utils import run_bass_kernel_spmd

    nc = bacc.Bacc("TRN2", target_bir_lowering=False, num_devices=1)
    arrays, t = {}, {}
    for name, value in inputs.items():
        a = np.ascontiguousarray(value)
        arrays[f"in_{name}"] = a
        t[name] = nc.dram_tensor(f"in_{name}", a.shape, mybir.dt.from_np(a.dtype), kind="ExternalInput").ap()
    out = nc.dram_tensor("out_0", _OUT, F32, kind="ExternalOutput").ap()
    build(nc, t, out)
    return run_bass_kernel_spmd(nc, [arrays], core_ids=[0]).results[0]["out_0"]
```
